# Optimizing a Trainium2 kernel written in Bass

```python
import numpy as np
import jax
import jax.numpy as jnp

def _softmax(x, axis=-1):
    return jax.nn.softmax(x, axis=axis)

def _gelu(x):
    return jax.nn.gelu(x, approximate=True)

def _silu(x):
    return jax.nn.silu(x)

def _sigmoid(x):
    return jax.nn.sigmoid(x)

def _layernorm(x, axis=-1, eps=1e-05):
    m = jnp.mean(x, axis=axis, keepdims=True)
    v = jnp.var(x, axis=axis, keepdims=True)
    return (x - m) / jnp.sqrt(v + eps)

def _scatter_add(tgt, idx, src, axis=0):
    return tgt.at[idx].add(src)

def _segment_sum(src, seg, n):
    return jax.ops.segment_sum(src, seg, n)
kernel_name = 'mk_xattn_ffn_d1_seqx_r4_955240'

def setup_inputs(seed: int=0):
    np.random.seed(seed)
    _w = jnp.asarray

    def _rec_inputs():
        import jax
        import jax.numpy as jnp
        _rk = jax.random.key(seed)
        x = -0.0002928 + 1 * jax.random.normal(jax.random.fold_in(_rk, 1), (2, 1024, 256), jnp.float32)
        _lenS = 1024 - jax.random.randint(jax.random.fold_in(_rk, 7), (2,), 0, max(1, 1024 // 4) + 1, jnp.int32)
        _lenS2 = 77 - jax.random.randint(jax.random.fold_in(_rk, 8), (2,), 0, max(1, 77 // 4) + 1, jnp.int32)
        _ctx_1024P = jax.random.normal(jax.random.fold_in(_rk, 11), (2, 16, 256), jnp.float32)
        _ctx_1024c = jax.random.dirichlet(jax.random.fold_in(_rk, 511), 0.3 * jnp.ones((16,), jnp.float32), (2, 77))
        _ctx_1024t = jnp.einsum('bsk,bkd->bsd', _ctx_1024c, _ctx_1024P)
        _ctx_1024t = _ctx_1024t * jax.lax.rsqrt(jnp.mean(jnp.square(_ctx_1024t)) + 1e-12) * 0.953939
        ctx_1024 = -1.39393e-06 + 0.999914 * (_ctx_1024t + 0.3 * jax.random.normal(jax.random.fold_in(_rk, 611), (2, 77, 256), jnp.float32))
        _validS = jnp.arange(1024)[None, :] < _lenS[:, None]
        _validS2 = jnp.arange(77)[None, :] < _lenS2[:, None]
        _causal = jnp.tril(jnp.ones((1024, 1024), dtype=bool))
        mask_1x1xSxS2_fk0 = jnp.where(jnp.broadcast_to(_validS2[0:1, None, None, :], (1, 1, 1024, 77)), 0.0, 1.0).astype(jnp.float32)
        return (x, ctx_1024, mask_1x1xSxS2_fk0)
    x, ctx_1024, mask_1x1xSxS2_fk0 = _rec_inputs()

    def _L0_xattn_setup():
        import jax, jax.numpy as jnp
        import numpy as np
        B, T, E, H = (2, 512, 256, 16)
        key = jax.random.key(seed)
        ks = jax.random.split(key, 8)
        std = 1.0 / np.sqrt(E)
        x = jax.random.normal(ks[0], (B, T, E), dtype=jnp.float32)
        y = jax.random.normal(ks[1], (B, T, E), dtype=jnp.float32)
        mask = jnp.tril(jnp.ones((T, T), dtype=jnp.float32))[None, None]
        Wq = jax.random.normal(ks[2], (E, E), dtype=jnp.float32) * std
        Wk = jax.random.normal(ks[3], (E, E), dtype=jnp.float32) * std
        Wv = jax.random.normal(ks[4], (E, E), dtype=jnp.float32) * std
        Wo = jax.random.normal(ks[5], (E, E), dtype=jnp.float32) * std
        bq = jnp.zeros((E,), jnp.float32)
        bk = jnp.zeros((E,), jnp.float32)
        bv = jnp.zeros((E,), jnp.float32)
        bo = jnp.zeros((E,), jnp.float32)
        return {'x': x, 'y': y, 'mask': mask, 'Wq': Wq, 'bq': bq, 'Wk': Wk, 'bk': bk, 'Wv': Wv, 'bv': bv, 'Wo': Wo, 'bo': bo, 'num_heads': H}
    _L0_xattn_all = _L0_xattn_setup()
    _L0_xattn_in = {k: v for k, v in _L0_xattn_all.items() if k in ('Wq', 'bq', 'Wk', 'bk', 'Wv', 'bv', 'Wo', 'bo')}
    del _L0_xattn_all

    def _L0_ffn_setup():
        import jax, jax.numpy as jnp
        import numpy as np
        B, S, D, F, E = (2, 512, 256, 1024, 8)
        LN_EPS = 1e-05

        def _xavier(key, shape, fan_in, fan_out):
            a = np.sqrt(6.0 / (fan_in + fan_out))
            return jax.random.uniform(key, shape, jnp.float32, -a, a)
        key = jax.random.key(seed)
        ks = jax.random.split(key, 8)
        tgt = jax.random.normal(ks[0], (B, S, D), jnp.float32)
        router_w = _xavier(ks[1], (E, D), D, E)
        router_b = jnp.zeros((E,), jnp.float32)
        w1 = _xavier(ks[2], (E, D, F), D, F)
        b1 = jnp.zeros((E, F), jnp.float32)
        w2 = _xavier(ks[3], (E, F, D), F, D)
        b2 = jnp.zeros((E, D), jnp.float32)
        gamma = jnp.ones((D,), jnp.float32)
        beta = jnp.zeros((D,), jnp.float32)
        return {'tgt': tgt, 'router_w': router_w, 'router_b': router_b, 'w1': w1, 'b1': b1, 'w2': w2, 'b2': b2, 'gamma': gamma, 'beta': beta}
    _L0_ffn_all = _L0_ffn_setup()
    _L0_ffn_in = {k: v for k, v in _L0_ffn_all.items() if k in ('router_w', 'router_b', 'w1', 'b1', 'w2', 'b2', 'gamma', 'beta')}
    del _L0_ffn_all
    return {'x': x, 'ctx_1024': ctx_1024, 'mask_1x1xSxS2_fk0': mask_1x1xSxS2_fk0, 'L0_xattn_Wq': _L0_xattn_in['Wq'], 'L0_xattn_bq': _L0_xattn_in['bq'], 'L0_xattn_Wk': _L0_xattn_in['Wk'], 'L0_xattn_bk': _L0_xattn_in['bk'], 'L0_xattn_Wv': _L0_xattn_in['Wv'], 'L0_xattn_bv': _L0_xattn_in['bv'], 'L0_xattn_Wo': _L0_xattn_in['Wo'], 'L0_xattn_bo': _L0_xattn_in['bo'], 'L0_ffn_router_w': _L0_ffn_in['router_w'], 'L0_ffn_router_b': _L0_ffn_in['router_b'], 'L0_ffn_w1': _L0_ffn_in['w1'], 'L0_ffn_b1': _L0_ffn_in['b1'], 'L0_ffn_w2': _L0_ffn_in['w2'], 'L0_ffn_b2': _L0_ffn_in['b2'], 'L0_ffn_gamma': _L0_ffn_in['gamma'], 'L0_ffn_beta': _L0_ffn_in['beta']}

def reference(x, ctx_1024, mask_1x1xSxS2_fk0, L0_xattn_Wq, L0_xattn_bq, L0_xattn_Wk, L0_xattn_bk, L0_xattn_Wv, L0_xattn_bv, L0_xattn_Wo, L0_xattn_bo, L0_ffn_router_w, L0_ffn_router_b, L0_ffn_w1, L0_ffn_b1, L0_ffn_w2, L0_ffn_b2, L0_ffn_gamma, L0_ffn_beta):
    import jax
    import jax.numpy as jnp

    def _L0_xattn_ref(x, y, mask, Wq, bq, Wk, bk, Wv, bv, Wo, bo, num_heads):
        import jax, jax.numpy as jnp
        import numpy as np
        B, T, E, H = (2, 512, 256, 16)
        Bx, Tq, Emb = x.shape
        Tkv = y.shape[1]
        d = Emb // num_heads
        q = (x @ Wq + bq).reshape(Bx, Tq, num_heads, d)
        k = (y @ Wk + bk).reshape(Bx, Tkv, num_heads, d)
        v = (y @ Wv + bv).reshape(Bx, Tkv, num_heads, d)
        scale = 1.0 / np.sqrt(d).astype(np.float32)
        att = scale * jnp.einsum('bthd,bThd->bhtT', q, k)
        att = att * mask - 10000000000.0 * (1.0 - mask)
        att = jax.nn.softmax(att, axis=-1)
        out = jnp.einsum('bhtT,bThd->bthd', att, v).reshape(Bx, Tq, Emb)
        return out @ Wo + bo

    def _L0_ffn_ref(tgt, router_w, router_b, w1, b1, w2, b2, gamma, beta):
        import jax, jax.numpy as jnp
        import numpy as np
        B, S, D, F, E = (2, 512, 256, 1024, 8)
        LN_EPS = 1e-05

        def _xavier(key, shape, fan_in, fan_out):
            a = np.sqrt(6.0 / (fan_in + fan_out))
            return jax.random.uniform(key, shape, jnp.float32, -a, a)
        logits = jnp.einsum('bsd,ed->bse', tgt, router_w) + router_b
        rw = jax.nn.softmax(logits, axis=-1)
        rw = jnp.zeros_like(rw).at[..., 0].set(1.0)
        h = jax.nn.relu(jnp.einsum('bsd,edf->besf', tgt, w1) + b1[None, :, None, :])
        eo = jnp.einsum('besf,efd->besd', h, w2) + b2[None, :, None, :]
        tgt2 = jnp.einsum('besd,bse->bsd', eo, rw)
        x = tgt + tgt2
        mean = jnp.mean(x, axis=-1, keepdims=True)
        var = jnp.mean(jnp.square(x - mean), axis=-1, keepdims=True)
        return (x - mean) * jax.lax.rsqrt(var + LN_EPS) * gamma + beta
    x = x + _L0_xattn_ref(_layernorm(x, axis=-1), ctx_1024, mask_1x1xSxS2_fk0, L0_xattn_Wq, L0_xattn_bq, L0_xattn_Wk, L0_xattn_bk, L0_xattn_Wv, L0_xattn_bv, L0_xattn_Wo, L0_xattn_bo, 16)
    x = x + _L0_ffn_ref(_layernorm(x, axis=-1), L0_ffn_router_w, L0_ffn_router_b, L0_ffn_w1, L0_ffn_b1, L0_ffn_w2, L0_ffn_b2, L0_ffn_gamma, L0_ffn_beta)
    return x

_drawn_inputs = setup_inputs


def setup_inputs(seed=0):
    import zlib

    import numpy as np

    out = dict(_drawn_inputs(seed))
    spreads = {'L0_xattn_bq': (0.0, 0.414),
     'L0_xattn_bk': (0.0, 0.8),
     'L0_xattn_bv': (0.0, 0.1),
     'L0_xattn_bo': (0.0, 0.1),
     'L0_ffn_router_b': (0.0, 0.1),
     'L0_ffn_b1': (0.0, 0.1),
     'L0_ffn_b2': (0.0, 0.1),
     'L0_ffn_gamma': (1.0, 0.2),
     'L0_ffn_beta': (0.0, 0.1)}
    factors = {}
    for name, (base, spread) in spreads.items():
        noise = np.random.default_rng([zlib.crc32(name.encode()), seed]).standard_normal(out[name].shape)
        drawn = base * np.exp(spread * noise) if base else spread * noise
        out[name] = jnp.asarray(drawn.astype(out[name].dtype))
    for name, factor in factors.items():
        out[name] = (out[name] * factor).astype(out[name].dtype)
    return out
```

```python
from contextlib import ExitStack

import numpy as np
import concourse.bass as bass
from concourse import mybir

F32 = mybir.dt.float32
F32R = mybir.dt.float32r
BF16 = mybir.dt.bfloat16
ALU = mybir.AluOpType
ACT = mybir.ActivationFunctionType
AX_X = mybir.AxisListType.X

P = 128
E = 256
NT = 16
NC = 4
H = 16
D = 16
TK = 77
F = 1024
G = 8 * TK
EPS = 1e-5
BIG = float(2.0 ** 60)
KROWS = [128, 128, 128, 128, G - 512]


class Engine:

    def __init__(self, sem):
        self.sem, self.count, self.queue, self.seen = sem, 0, [], {}

    def wait(self, *marks):
        for sem, value in marks:
            if self.seen.get(sem.name, 0) < value:
                self.seen[sem.name] = value
                self.queue.append(lambda e, sem=sem, value=value: e.wait_ge(sem, value))

    def run(self, what):
        self.queue.append(what)

    def done(self, what):
        self.count += 1
        self.queue.append(lambda e: what(e).then_inc(self.sem, 1))
        return (self.sem, self.count)

    def play(self, e):
        for what in self.queue:
            what(e)


class Banks:

    def __init__(self, pe, tensors):
        self.pe, self.tensors, self.at, self.read = pe, tensors, 0, [None] * len(tensors)

    def take(self):
        n = self.at % len(self.tensors)
        self.at += 1
        if self.read[n] is not None:
            self.pe.wait(self.read[n])
        return n, self.tensors[n]

    def free(self, n, mark):
        self.read[n] = mark


def build(nc, x, ctx_in, mask, Wq, bq, Wk, bk, Wv, bv, Wo, bo, w1, b1, w2, b2, gamma, beta, const, out):
    stack = ExitStack()
    with stack:
        def sb(name, shape, dt=F32):
            return stack.enter_context(nc.sbuf_tensor(name, shape, dt))

        def ps(name, shape, dt=F32):
            return stack.enter_context(nc.psum_tensor(name, shape, dt))

        def sem(name):
            return stack.enter_context(nc.semaphore(name))

        cst = sb("cst", [P, 176])
        ident = cst[:, 0:128]
        bmask = cst[:, 128:136]
        vmask = cst[:, 136:176]
        rep = sb("rep", [TK, 4 * TK])
        repb = sb("repb", [TK, 4 * TK], BF16)
        identb = sb("identb", [P, P], BF16)
        mrow = sb("mrow", [P, 8, TK])
        crow = sb("crow", [P, 8, TK], BF16)
        cT = sb("cT", [TK, 1024], BF16)
        rows = sb("rows", [14, P])
        cols = sb("cols", [P, 14])
        bq4 = sb("bq4", [P, 2])
        bo_r = sb("bo_r", [P, E])
        b2_r = sb("b2_r", [P, E])
        ga_r = sb("ga_r", [P, E])
        be_r = sb("be_r", [P, E])
        wq = sb("wq", [P, 2, E])
        wk = sb("wk", [P, 2, E])
        wv = sb("wv", [P, 2, E])
        wo = sb("wo", [P, 2, E])
        ctx = sb("ctx", [TK, 2, E])
        ctxT = sb("ctxT", [P, 2, 2, TK])
        kT = sb("kT", [P, 2, 2 * TK])
        vsb = sb("vsb", [TK, 2, E])
        Kb = sb("Kb", [P, 2, 2, G])
        Vb = sb("Vb", [P, 2, 5, E])
        w1h = sb("w1h", [P, 2048], F32R)
        w1l = sb("w1l", [P, 2048], F32R)
        w2h = sb("w2h", [P, 2048], F32R)
        w2l = sb("w2l", [P, 2048], F32R)
        xin = sb("xin", [P, NT, E])
        xn = sb("xn", [P, 4, E])
        xnT = sb("xnT", [P, 2, 512])
        qT = sb("qT", [P, 2, 2, 512])
        Pm = sb("Pm", [P, 4, 2, G])
        PT = sb("PT", [P, 3, 512])
        aT = sb("aT", [P, 2, 512])
        x1 = sb("x1", [P, 2, 4, E])
        xn2 = sb("xn2", [P, 2, 4, E])
        w1raw = xn2[:, :, :, :].rearrange("p a n e -> p (a n e)")
        w2raw = x1[:, :, :, :].rearrange("p a n e -> p (a n e)")
        x2h = sb("x2h", [P, 2, 512], F32R)
        x2l = sb("x2l", [P, 2, 512], F32R)
        hr = sb("hr", [P, 2, 512])
        hh = sb("hh", [P, 8, 512], F32R)
        hl = sb("hl", [P, 8, 512], F32R)
        yb = sb("yb", [P, 2, 2, E])
        mx = sb("mx", [P, 2, 8])
        dn = sb("dn", [P, 2, 8])
        rd = sb("rd", [P, 2, 8])
        st = sb("st", [P, 4, 6])
        mv = sb("mv", [P, 4, 2])
        ve = sb("ve", [P, 4])
        rs = sb("rs", [P, 4])
        mh = sb("mh", [P, 4])

        S = [ps("S0", [P, 2, 512]), ps("S1", [P, 2, 512])]
        W = [ps(f"W{i}", [P, 512]) for i in range(4)]

        pe = Engine(sem("pe_done"))
        dve = Engine(sem("dve_done"))
        act = Engine(sem("act_done"))
        pool = Engine(sem("pool_done"))
        sp = Engine(sem("sp_done"))
        bank = Banks(pe, W)

        def load(name, dst, src, eng=sp):
            s = sem("ld_" + name)
            eng.run(lambda e: e.dma_start(dst, src).then_inc(s, 16))
            return (s, 16)

        def wview(w):
            return w.rearrange("(k p) n -> p k n", p=P)

        def row_all(v):
            return v.partition_broadcast(P)

        x_v = x.rearrange("b (n p) e -> p (b n) e", p=P)
        o_v = out.rearrange("b (n p) e -> p (b n) e", p=P)

        ld_c = load("c", cst[:, :], const)
        ld_x = [load("x0", xin[:, 0:4, :], x_v[:, 0:4, :])]
        ld_ctx = load("ctx", ctx[:, :, :], ctx_in.rearrange("b t e -> t b e"), act)
        s_rows = sem("ld_rows")
        for r0, n, v in ((0, 2, bq), (2, 2, bk), (4, 2, bv), (6, 8, b1[0, :])):
            act.run(lambda e, r0=r0, n=n, v=v: e.dma_start(
                rows[r0:r0 + n, :], v.rearrange("(k p) -> k p", p=P)).then_inc(s_rows, 16))
        ld_rows = (s_rows, 64)
        ld_wk = load("wk", wk[:, :, :], wview(Wk), act)
        ld_wq = load("wq", wq[:, :, :], wview(Wq))
        ld_wv = load("wv", wv[:, :, :], wview(Wv), act)
        ld_m = load("m", mrow[:, :, :], mask[0, 0].rearrange("(n p) t -> p n t", p=P))
        ld_bo = load("bo", bo_r[:, :], row_all(bo))
        ld_wo = load("wo", wo[:, :, :], wview(Wo))
        ld_w1 = load("w1", w1raw.rearrange("p (k n) -> p k n", k=2), wview(w1[0]))
        ld_w2 = load("w2", w2raw.rearrange("p (k n) -> p k n", k=8), wview(w2[0]))
        ld_x.append(load("x1", xin[:, 4:8, :], x_v[:, 4:8, :]))
        ld_b2 = load("b2", b2_r[:, :], row_all(b2[0]))
        ld_ga = load("ga", ga_r[:, :], row_all(gamma))
        ld_be = load("be", be_r[:, :], row_all(beta))
        ld_x.append(load("x2", xin[:, 8:12, :], x_v[:, 8:12, :]))
        ld_x.append(load("x3", xin[:, 12:16, :], x_v[:, 12:16, :]))

        dve.wait(ld_c)
        t_idb = dve.done(lambda e: e.tensor_copy(identb[:, :], ident))
        id77 = cst[0:TK, 0:TK].unsqueeze(1).to_broadcast([TK, 4, TK])
        t_rep = dve.done(lambda e: e.tensor_copy(rep[:, :].rearrange("p (r t) -> p r t", t=TK), id77))
        t_repb = dve.done(lambda e: e.tensor_copy(repb[:, :].rearrange("p (r t) -> p r t", t=TK), id77))
        t_mh = pool.done(lambda e: e.memset(mh[:, :], -0.5))

        def rstd(marks, free_rs):
            dve.wait(*marks)
            for n in range(4):
                m = dve.done(lambda e, n=n: e.bn_aggr(mv[:, n, :], st[:, n, :]))
            dve.wait(m)
            m = dve.done(lambda e: e.tensor_scalar(ve[:, :], mv[:, :, 1], EPS, None, ALU.add))
            pool.wait(m, t_mh)
            return pool.done(lambda e: e.tensor_tensor(rs[:, :], ve[:, :], mh[:, :], ALU.pow))

        t_xnT = [None] * NC
        t_qT = [None] * NC
        t_xb = [None] * NC
        t_xnc = [None] * NC
        last = {"xn_read": [], "xnT_read": [], "qT_read": {}, "stat": None, "P_read": [], "aT_read": [],
                "xb_read": {}, "x1_read": {}, "xn2_read": {}, "x2_read": [], "h_read": [], "yb_read": {},
                "ob_read": {}, "xn2b_read": {}, "x1b_read": {}, "PT_read": {}, "hr_read": {}, "S_read": {},
                "rd": {}}

        def norm1(c):
            dve.wait(ld_x[c])
            for n in range(4):
                m = dve.done(lambda e, n=n: e.bn_stats(st[:, n, :], xin[:, 4 * c + n, :]))
            r = rstd([m], None)
            dve.wait(r, *last["xn_read"])
            for n in range(4):
                m = dve.done(lambda e, n=n: e.tensor_scalar(
                    xn[:, n, :], xin[:, 4 * c + n, :], mv[:, n, 0:1], rs[:, n:n + 1], ALU.subtract, ALU.mult))
            t_xnc[c] = [m]
            pe.wait(m, ld_c)
            for k in range(2):
                b, t = bank.take()
                for n in range(4):
                    f = lambda e, n=n, t=t, k=k: e.transpose(t[:, n * 128:(n + 1) * 128], xn[:, n, k * 128:(k + 1) * 128], ident)
                    m = pe.done(f) if n == 3 else pe.run(f)
                act.wait(m, *last["xnT_read"])
                a = act.done(lambda e, t=t, k=k: e.copy(xnT[:, k, :], t[:, :]))
                bank.free(b, a)
            last["xn_read"] = [m]
            t_xnT[c] = a

        def xbias(c):
            pool.wait(ld_bo, *t_xnc[c])
            for n in range(4):
                t_xb[c] = pool.done(lambda e, n=n: e.tensor_tensor(xin[:, 4 * c + n, :], xin[:, 4 * c + n, :], bo_r[:, :], ALU.add))

        def qproj(c):
            pe.wait(t_xnT[c], ld_wq)
            for m_ in range(2):
                b, t = bank.take()
                pe.run(lambda e, t=t, m_=m_: e.matmul(t[:, :], wq[:, 0, m_ * 128:(m_ + 1) * 128], xnT[:, 0, :], start=True, stop=False))
                m = pe.done(lambda e, t=t, m_=m_: e.matmul(t[:, :], wq[:, 1, m_ * 128:(m_ + 1) * 128], xnT[:, 1, :], start=False, stop=True))
                act.wait(m, t_bq4, *last["qT_read"].get(c % 2, []))
                a = act.done(lambda e, t=t, m_=m_: e.activation(qT[:, c % 2, m_, :], t[:, :], ACT.Identity, bias=bq4[:, m_:m_ + 1], scale=0.25))
                bank.free(b, a)
            last["xnT_read"] = [m]
            t_qT[c] = a

        pe.wait(ld_rows, ld_c)
        b, t = bank.take()
        m = pe.done(lambda e, t=t: e.transpose(t[:, 0:14], rows[:, :], cst[0:14, 0:14]))
        dve.wait(m)
        t_cols = dve.done(lambda e, t=t: e.tensor_copy(cols[:, :], t[:, 0:14]))
        bank.free(b, t_cols)
        dve.wait(t_cols)
        t_bq4 = dve.done(lambda e: e.tensor_scalar(bq4[:, :], cols[:, 0:2], 0.25, None, ALU.mult))

        norm1(0)
        qproj(0)
        xbias(0)

        pe.wait(ld_ctx)
        b, t = bank.take()
        for bb in range(2):
            for k in range(2):
                m = pe.done(lambda e, t=t, bb=bb, k=k: e.transpose(
                    t[:, (2 * k + bb) * TK:(2 * k + bb + 1) * TK], ctx[:, bb, k * 128:(k + 1) * 128], cst[0:TK, 0:TK]))
        act.wait(m)
        t_ctxT = act.done(lambda e, t=t: e.copy(ctxT[:, :, :, :].rearrange("p k b t -> p (k b t)"), t[:, 0:4 * TK]))
        bank.free(b, t_ctxT)
        pe.wait(t_ctxT, ld_wk)
        t_Kb = {}
        for g in range(2):
            b, t = bank.take()
            for k in range(2):
                f = lambda e, t=t, g=g, k=k: e.matmul(
                    t[:, 0:2 * TK], wk[:, k, g * 128:(g + 1) * 128], ctxT[:, k, :, :].rearrange("p b t -> p (b t)"),
                    start=(k == 0), stop=(k == 1))
                m = pe.done(f) if k else pe.run(f)
            act.wait(m, t_cols)
            a = act.done(lambda e, t=t, g=g: e.activation(kT[:, g, :], t[:, 0:2 * TK], ACT.Identity, bias=cols[:, 2 + g:3 + g]))
            bank.free(b, a)
            dve.wait(a)
            for bb in range(2):
                t_Kb[bb, g] = dve.done(lambda e, g=g, bb=bb: e.tensor_tensor(
                    Kb[:, bb, g, :].rearrange("p (h t) -> p h t", t=TK),
                    kT[:, g, bb * TK:(bb + 1) * TK].unsqueeze(1).to_broadcast([P, 8, TK]),
                    bmask.unsqueeze(2).to_broadcast([P, 8, TK]), ALU.mult))
        dve.wait(ld_m)
        m = dve.done(lambda e: e.tensor_scalar(crow[:, :, :], mrow[:, :, :], 1.0, BIG, ALU.subtract, ALU.mult))
        pe.wait(m, t_idb)
        b, t = bank.take()
        tb = t[:, :].bitcast(BF16)
        for n in range(8):
            f = lambda e, tb=tb, n=n: e.transpose(tb[0:TK, n * 128:(n + 1) * 128], crow[:, n, :], identb[:, :])
            m = pe.done(f) if n == 7 else pe.run(f)
        dve.wait(m)
        t_cT = dve.done(lambda e, tb=tb: e.tensor_copy(cT[:, :], tb[0:TK, :]))
        bank.free(b, t_cT)

        def values():
            pe.wait(t_ctxT, ld_wv)
            marks = []
            for bb in range(2):
                b, t = bank.take()
                for k in range(2):
                    f = lambda e, t=t, bb=bb, k=k: e.matmul(t[0:TK, 0:E], ctxT[:, k, bb, :], wv[:, k, :], start=(k == 0), stop=(k == 1))
                    m = pe.done(f) if k else pe.run(f)
                act.wait(m)
                a = act.done(lambda e, t=t, bb=bb: e.copy(vsb[:, bb, :], t[0:TK, 0:E]))
                bank.free(b, a)
                marks.append(a)
            for bb in range(2):
                for j in range(5):
                    pe.wait(marks[bb], t_rep)
                    b, t = bank.take()
                    o = 128 * j % TK
                    m = pe.done(lambda e, t=t, bb=bb, o=o: e.matmul(t[:, 0:E], rep[:, o:o + 128], vsb[:, bb, :], start=True, stop=True))
                    dve.wait(m)
                    a = dve.done(lambda e, t=t, bb=bb, j=j: e.tensor_tensor(
                        Vb[:, bb, j, :].rearrange("p (g h d) -> p g h d", g=2, d=D),
                        t[:, 0:E].rearrange("p (g h d) -> p g h d", g=2, d=D),
                        vmask[:, 8 * j:8 * j + 8].unsqueeze(1).unsqueeze(3).to_broadcast([P, 2, 8, D]), ALU.mult))
                    bank.free(b, a)
            return a

        def split(raw, hi, lo, loaded):
            act.wait(loaded)
            a = act.done(lambda e: e.copy(hi[:, :], raw))
            pool.wait(a)
            return pool.done(lambda e: e.tensor_tensor(lo[:, :], raw, hi[:, :].bitcast(F32), ALU.subtract))

        t_P = {}
        units = [0]

        def scores(i, g):
            c, n, bb = i // 4, i % 4, i // 8
            u = units[0] % 2
            units[0] += 1
            s = S[u]
            pe.wait(t_qT[c], t_Kb[bb, g], t_cT, t_repb, *last["S_read"].get(u, []))
            for h in range(2):
                pe.run(lambda e, h=h: e.matmul(s[:, h, 0:4 * TK], qT[:, c % 2, g, n * 128:(n + 1) * 128],
                                               Kb[:, bb, g, h * 4 * TK:(h + 1) * 4 * TK], start=True, stop=False))
            q0 = (i % 8) * 128
            for h in range(2):
                f = lambda e, h=h: e.matmul(s[:, h, 0:4 * TK], cT[:, q0:q0 + 128], repb[:, :], start=False, stop=True)
                m = pe.done(f) if h else pe.run(f)
            last["qT_read"][c % 2] = [m]
            sv = s[:, :, 0:4 * TK].rearrange("p b (h t) -> p b h t", t=TK)
            pm = Pm[:, n, g, :]
            p3 = pm.rearrange("p (h t) -> p h t", t=TK)
            dve.wait(m)
            m = dve.done(lambda e: e.tensor_reduce(mx[:, u, :].rearrange("p (b h) -> p b h", b=2), sv, AX_X, ALU.max))
            dve.wait(m, *last["P_read"])
            m = dve.done(lambda e: e.tensor_tensor(
                pm.rearrange("p (b h t) -> p b h t", b=2, t=TK), sv,
                mx[:, u, :].rearrange("p (b h) -> p b h", b=2).unsqueeze(3).to_broadcast([P, 2, 4, TK]), ALU.subtract))
            last["S_read"][u] = [m]
            act.wait(m)
            a = act.done(lambda e: e.activation(pm, pm, ACT.Exp))

            def rest():
                dve.wait(a)
                m = dve.done(lambda e: e.tensor_reduce(dn[:, u, :], p3, AX_X, ALU.add))
                dve.wait(m, *last["rd"].get(u, []))
                m = dve.done(lambda e: e.reciprocal(rd[:, u, :], dn[:, u, :]))
                pool.wait(m)
                t_P[i, g] = pool.done(lambda e: e.tensor_tensor(p3, p3, rd[:, u, :].unsqueeze(2).to_broadcast([P, 8, TK]), ALU.mult))
                last["rd"][u] = [t_P[i, g]]
            return rest

        t_aT = {}

        def values_sum(c):
            bb = c // 2
            pts = [0]
            for g in range(2):
                acc_b, acc = bank.take()
                pend = []

                def pv(j, slot, a, g=g, acc=acc):
                    pe.wait(a, t_Vb)
                    m = pe.done(lambda e: e.matmul(acc[:, :], Vb[0:KROWS[j], bb, j, g * 128:(g + 1) * 128],
                                                     PT[0:KROWS[j], slot, :], start=(j == 0), stop=(j == 4)))
                    last["PT_read"][slot] = [m]
                    return m
                for j in range(5):
                    r = KROWS[j]
                    b, t = bank.take() if j != 4 or True else None
                    for n in range(4):
                        pe.wait(t_P[4 * c + n, g])
                        f = lambda e, n=n, t=t, r=r, j=j, g=g: e.transpose(t[0:r, n * 128:(n + 1) * 128], Pm[:, n, g, j * 128:j * 128 + r], ident)
                        m = pe.done(f) if n == 3 else pe.run(f)
                    slot = pts[0] % 3
                    pts[0] += 1
                    act.wait(m, *last["PT_read"].get(slot, []))
                    a = act.done(lambda e, t=t, r=r, slot=slot: e.copy(PT[0:r, slot, :], t[0:r, :]))
                    bank.free(b, a)
                    pend.append((j, slot, a))
                    if len(pend) > 1:
                        pv(*pend.pop(0))
                    if bank.at % 4 == acc_b:
                        bank.at += 1
                last_t = m
                mm = pv(*pend.pop(0))
                act.wait(mm, *last["aT_read"])
                a = act.done(lambda e, g=g, acc=acc: e.activation(aT[:, g, :], acc[:, :], ACT.Identity, bias=cols[:, 4 + g:5 + g]))
                bank.free(acc_b, a)
            last["P_read"] = [last_t]
            t_aT[c] = a

        t_x2 = {}

        def out_norm2(c):
            pe.wait(t_aT[c], ld_wo)
            for h in range(2):
                b, t = bank.take()
                for n in range(2):
                    q = (2 * h + n) * 128
                    for k in range(2):
                        f = lambda e, t=t, n=n, q=q, k=k: e.matmul(t[:, n * E:(n + 1) * E], aT[:, k, q:q + 128], wo[:, k, :],
                                                                   start=(k == 0), stop=(k == 1))
                        m = pe.done(f) if n and k else pe.run(f)
                dve.wait(m, t_xb[c], t_w2, *last["x1_read"].get(c % 2, []))
                d = dve.done(lambda e, t=t, h=h: e.tensor_tensor(
                    x1[:, c % 2, 2 * h:2 * h + 2, :].rearrange("p n e -> p (n e)"), t[:, :],
                    xin[:, 4 * c + 2 * h:4 * c + 2 * h + 2, :].rearrange("p n e -> p (n e)"), ALU.add))
                bank.free(b, d)
                dve.wait(d)
                for n in range(2):
                    s = dve.done(lambda e, h=h, n=n: e.bn_stats(st[:, 2 * h + n, :], x1[:, c % 2, 2 * h + n, :]))
            last["aT_read"] = [m]
            r = rstd([s], None)
            dve.wait(r, t_w1, *last["xn2_read"].get(c % 2, []))
            for n in range(4):
                m = dve.done(lambda e, n=n: e.tensor_scalar(xn2[:, c % 2, n, :], x1[:, c % 2, n, :], mv[:, n, 0:1], rs[:, n:n + 1], ALU.subtract, ALU.mult))
            pe.wait(m)
            t_n2 = m
            for k in range(2):
                b, t = bank.take()
                for n in range(4):
                    f = lambda e, n=n, t=t, k=k: e.transpose(t[:, n * 128:(n + 1) * 128], xn2[:, c % 2, n, k * 128:(k + 1) * 128], ident)
                    m = pe.done(f) if n == 3 else pe.run(f)
                act.wait(m, *last["x2_read"])
                a = act.done(lambda e, t=t, k=k: e.copy(x2h[:, k, :], t[:, :]))
                dve.wait(a)
                d = dve.done(lambda e, t=t, k=k: e.tensor_tensor(x2l[:, k, :], t[:, :], x2h[:, k, :].bitcast(F32), ALU.subtract))
                bank.free(b, d)
            t_x2[c] = d
            pool.wait(t_n2, m, ld_b2, ld_be)
            for n in range(4):
                pool.run(lambda e, n=n: e.tensor_tensor(xn2[:, c % 2, n, :], xn2[:, c % 2, n, :], b2_r[:, :], ALU.add))
                p = pool.done(lambda e, n=n: e.tensor_tensor(x1[:, c % 2, n, :], x1[:, c % 2, n, :], be_r[:, :], ALU.add))
            t_x1b[c] = p

        t_x1b = {}
        t_h = {}

        def ffn1(c, f_):
            pe.wait(t_x2[c], t_w1)
            b, t = bank.take()
            n = 0
            for k in range(2):
                o = k * F + f_ * 128
                for w, y in ((w1h, x2h), (w1h, x2l), (w1l, x2h)):
                    f = lambda e, w=w, y=y, n=n, o=o, k=k, t=t: e.matmul(t[:, :], w[:, o:o + 128], y[:, k, :], start=(n == 0), stop=(n == 5))
                    m = pe.done(f) if n == 5 else pe.run(f)
                    n += 1
            if f_ == 7:
                last["x2_read"] = [m]
            r = f_ % 2
            act.wait(m, *last["hr_read"].get(r, []))
            a = act.done(lambda e, t=t, r=r: e.activation(hr[:, r, :], t[:, :], ACT.Relu, bias=cols[:, 6 + f_:7 + f_]))
            bank.free(b, a)
            dve.wait(a, *last["h_read"])
            d = dve.done(lambda e, r=r: e.tensor_copy(hh[:, f_, :], hr[:, r, :]))
            dve.wait(d)
            d = dve.done(lambda e, r=r: e.tensor_tensor(hl[:, f_, :], hr[:, r, :], hh[:, f_, :].bitcast(F32), ALU.subtract))
            last["hr_read"][r] = [d]
            t_h[c] = d

        s_out = [sem("stored0"), sem("stored1")]
        stores = [0, 0]

        def ffn2(c, h):
            pe.wait(t_h[c], t_w2)
            b, t = bank.take()
            for n in range(2):
                q = (2 * h + n) * 128
                cnt = 0
                for f_ in range(8):
                    for y, w in ((hh, w2h), (hh, w2l), (hl, w2h)):
                        f = lambda e, y=y, w=w, f_=f_, q=q, n=n, cnt=cnt, t=t: e.matmul(
                            t[:, n * E:(n + 1) * E], y[:, f_, q:q + 128], w[:, f_ * E:(f_ + 1) * E], start=(cnt == 0), stop=(cnt == 23))
                        m = pe.done(f) if n and cnt == 23 else pe.run(f)
                        cnt += 1
            if h == 1:
                last["h_read"] = [m]
            u = h

            def rest():
                dve.wait(m, t_x1b[c], *last["ob_read"].get(u, []))
                d = dve.done(lambda e: e.tensor_tensor(
                    yb[:, u, :, :].rearrange("p n e -> p (n e)"), t[:, :],
                    xn2[:, c % 2, 2 * h:2 * h + 2, :].rearrange("p n e -> p (n e)"), ALU.add))
                bank.free(b, d)
                last["xn2_read"][c % 2] = [d]
                dve.wait(d)
                for n in range(2):
                    s = dve.done(lambda e, n=n: e.bn_stats(st[:, n, :], yb[:, u, n, :]))
                dve.wait(s)
                for n in range(2):
                    s = dve.done(lambda e, n=n: e.bn_aggr(mv[:, n, :], st[:, n, :]))
                dve.wait(s)
                s = dve.done(lambda e: e.tensor_scalar(ve[:, 0:2], mv[:, 0:2, 1], EPS, None, ALU.add))
                pool.wait(s, t_mh)
                s = pool.done(lambda e: e.tensor_tensor(rs[:, 0:2], ve[:, 0:2], mh[:, 0:2], ALU.pow))
                dve.wait(s)
                for n in range(2):
                    s = dve.done(lambda e, n=n: e.tensor_scalar(yb[:, u, n, :], yb[:, u, n, :], mv[:, n, 0:1], rs[:, n:n + 1], ALU.subtract, ALU.mult))
                dve.wait(s, ld_ga)
                gb = ga_r[:, :].unsqueeze(1).to_broadcast([P, 2, E])
                s = dve.done(lambda e: e.tensor_tensor(yb[:, u, :, :], yb[:, u, :, :], gb, ALU.mult))
                dve.wait(s)
                s = dve.done(lambda e: e.tensor_tensor(yb[:, u, :, :], yb[:, u, :, :], x1[:, c % 2, 2 * h:2 * h + 2, :], ALU.add))
                last["x1_read"][c % 2] = [s]
                sp.wait(s)
                n0 = 4 * c + 2 * h
                sp.run(lambda e: e.dma_start(o_v[:, n0:n0 + 2, :], yb[:, u, :, :]).then_inc(s_out[u], 16))
                stores[u] += 1
                last["ob_read"][u] = [(s_out[u], 16 * stores[u])]
            rest()

        t_w1 = t_w2 = None
        for c in range(NC):
            pend = None
            for n in range(4):
                for g in range(2):
                    r = scores(4 * c + n, g)
                    if pend:
                        pend()
                    pend = r
                    if c:
                        ffn1(c - 1, 2 * n + g)
                if c == 0 and n == 0:
                    t_Vb = values()
                if c == 0 and n == 1:
                    t_w1 = split(w1raw, w1h, w1l, ld_w1)
            pend()
            if c == 0:
                t_w2 = split(w2raw, w2h, w2l, ld_w2)
            if c + 1 < NC:
                norm1(c + 1)
                qproj(c + 1)
                xbias(c + 1)
            if c:
                ffn2(c - 1, 0)
                ffn2(c - 1, 1)
            values_sum(c)
            out_norm2(c)
        for f_ in range(8):
            ffn1(NC - 1, f_)
        ffn2(NC - 1, 0)
        ffn2(NC - 1, 1)
        sp.wait(*((s_out[u], 16 * stores[u]) for u in range(2)))

        block = stack.enter_context(nc.Block())
        block.sync(sp.play)
        block.scalar(act.play)
        block.vector(dve.play)
        block.gpsimd(pool.play)
        block.tensor(pe.play)


_INS = ["x", "ctx_1024", "mask_1x1xSxS2_fk0", "L0_xattn_Wq", "L0_xattn_bq", "L0_xattn_Wk", "L0_xattn_bk",
        "L0_xattn_Wv", "L0_xattn_bv", "L0_xattn_Wo", "L0_xattn_bo", "L0_ffn_w1", "L0_ffn_b1", "L0_ffn_w2",
        "L0_ffn_b2", "L0_ffn_gamma", "L0_ffn_beta"]


def _constants():
    c = np.zeros((128, 176), np.float32)
    p = np.arange(128)
    c[p, p] = 1.0
    c[p, 128 + p // 16] = 1.0
    for j in range(5):
        h = (128 * j + p) // 77
        ok = h < 8
        c[p[ok], 136 + 8 * j + h[ok]] = 1.0
    return c


def kernel(**inputs):
    import numpy as _np
    import concourse.bacc as _bacc
    from concourse import mybir as _mybir
    from concourse.bass_utils import run_bass_kernel_spmd as _run

    nc = _bacc.Bacc("TRN2", target_bir_lowering=False, num_devices=1)
    arrays, args = {}, []
    for name in _INS + ["const"]:
        a = _constants() if name == "const" else _np.ascontiguousarray(inputs[name])
        arrays[f"in_{name}_dram"] = a
        args.append(nc.dram_tensor(f"in_{name}_dram", a.shape, _mybir.dt.from_np(a.dtype), kind="ExternalInput").ap())
    out = nc.dram_tensor("out_0_dram", (2, 1024, 256), F32, kind="ExternalOutput").ap()
    build(nc, *args, out)
    r = _run(nc, [arrays], core_ids=[0])
    return r.results[0]["out_0_dram"]
```

```python
from contextlib import ExitStack

import numpy as np
import concourse.bass as bass
from concourse import mybir

F32 = mybir.dt.float32
F32R = mybir.dt.float32r
BF16 = mybir.dt.bfloat16
ALU = mybir.AluOpType
ACT = mybir.ActivationFunctionType
AX_X = mybir.AxisListType.X

P = 128
E = 256
NT = 16
NC = 4
H = 16
D = 16
TK = 77
F = 1024
G = 8 * TK
A = [0.176, 0.4, 0.5, 0.779, 0, 1.0, 0.751, 1.684, 0.909, 0.0]
EPS = 1e-5
BIG = float(2.0 ** 60)
KROWS = [128, 128, 128, 128, G - 512]
B = [0.219, 1.227, 0.05, 1.411, 0.487, 0.161, 0.617, 1.146, 1.4, 0.743]



class Engine:

    def __init__(self, sem):
        self.sem, self.count, self.queue, self.seen = sem, 0, [], {}

    def wait(self, *marks):
        for sem, value in marks:
            if self.seen.get(sem.name, 0) < value:
                self.seen[sem.name] = value
                self.queue.append(lambda e, sem=sem, value=value: e.wait_ge(sem, value))

    def run(self, what):
        self.queue.append(what)

    def done(self, what):
        self.count += 1
        self.queue.append(lambda e: what(e).then_inc(self.sem, 1))
        return (self.sem, self.count)

    def play(self, e):
        for what in self.queue:
            what(e)


class Banks:

    def __init__(self, pe, tensors):
        self.pe, self.idle = pe, [(t, None) for t in tensors]

    def take(self):
        t, reader = self.idle.pop(0)
        if reader is not None:
            self.pe.wait(reader)
        return t

    def give(self, t, reader):
        self.idle.append((t, reader))


def build(nc, x, ctx_in, mask, Wq, bq, Wk, bk, Wv, bv, Wo, bo, w1, b1, w2, b2, gamma, beta, const, out):
    stack = ExitStack()
    with stack:
        def sb(name, shape, dt=F32):
            return stack.enter_context(nc.sbuf_tensor(name, shape, dt))

        def ps(name, shape, dt=F32):
            return stack.enter_context(nc.psum_tensor(name, shape, dt))

        def sem(name):
            return stack.enter_context(nc.semaphore(name))

        cst = sb("cst", [P, 176])
        ident = cst[:, 0:128]
        bmask = cst[:, 128:136]
        vmask = cst[:, 136:176]
        rep = sb("rep", [TK, 4 * TK])
        repb = sb("repb", [TK, 4 * TK], BF16)
        identb = sb("identb", [P, P], BF16)
        hr = sb("hr", [P, 2, 512])
        yb = sb("yb", [P, 2, 2, E])
        hr_all = hr[:, :, :].rearrange("p a n -> p (a n)")
        mrow = hr_all[:, 0:8 * TK].rearrange("p (n t) -> p n t", t=TK)
        kraw = hr_all[:, 8 * TK:12 * TK].rearrange("p (g n) -> p g n", g=2)
        ctx = yb[0:TK, 0, :, :]
        crow = sb("crow", [P, 8, TK], BF16)
        cT = sb("cT", [TK, 1024], BF16)
        rows = sb("rows", [14, P])
        cols = sb("cols", [P, 14])
        bk4 = sb("bk4", [P, 2])
        bo_r = sb("bo_r", [P, E])
        b2_r = sb("b2_r", [P, E])
        ga_r = sb("ga_r", [P, E])
        be_r = sb("be_r", [P, E])
        wq = sb("wq", [P, 2, E])
        wk = sb("wk", [P, 2, E])
        wv = sb("wv", [P, 2, E])
        wo = sb("wo", [P, 2, E])
        ctxT = sb("ctxT", [P, 2, 2, TK])
        kT = sb("kT", [P, 2, 2, 2, TK], F32R)
        vsb = sb("vsb", [TK, 2, E])
        Kb = sb("Kb", [P, 2, 2, G], F32R)
        Vb = sb("Vb", [P, 2, 5, E])
        w1h = sb("w1h", [P, 2048], F32R)
        w1l = sb("w1l", [P, 2048], F32R)
        w2h = sb("w2h", [P, 2048], F32R)
        w2l = sb("w2l", [P, 2048], F32R)
        xin = sb("xin", [P, NT, E])
        xn = sb("xn", [P, 4, E])
        xnT = sb("xnT", [P, 2, 512])
        qh = sb("qh", [P, 2, 512], F32R)
        ql = sb("ql", [P, 2, 512], F32R)
        Pm = sb("Pm", [P, 4, 2, G])
        PT = sb("PT", [P, 4, 512])
        aT = sb("aT", [P, 2, 512])
        x1 = sb("x1", [P, 2, 4, E])
        xn2 = sb("xn2", [P, 2, 4, E])
        w1raw = xn2[:, :, :, :].rearrange("p a n e -> p (a n e)")
        w2raw = x1[:, :, :, :].rearrange("p a n e -> p (a n e)")
        x2h = sb("x2h", [P, 2, 512], F32R)
        x2l = sb("x2l", [P, 2, 512], F32R)
        hh = sb("hh", [P, 8, 512], F32R)
        hl = sb("hl", [P, 8, 512], F32R)
        mx = sb("mx", [P, 2, 8])
        dn = sb("dn", [P, 2, 8])
        rd = sb("rd", [P, 2, 8])
        st = sb("st", [P, 4, 6])
        mv = sb("mv", [P, 4, 2])
        ve = sb("ve", [P, 4])
        rs = sb("rs", [P, 4])
        mh = sb("mh", [P, 4])

        S = [ps("S0", [P, 2, 512]), ps("S1", [P, 2, 512])]
        W = [ps(f"W{i}", [P, 512]) for i in range(4)]

        pe = Engine(sem("pe_done"))
        dve = Engine(sem("dve_done"))
        act = Engine(sem("act_done"))
        pool = Engine(sem("pool_done"))
        sp = Engine(sem("sp_done"))
        bank = Banks(pe, W[0:3])
        acc = W[3]

        def load(name, dst, src, eng=sp):
            s = sem("ld_" + name)
            eng.run(lambda e: e.dma_start(dst, src).then_inc(s, 16))
            return (s, 16)

        def wview(w):
            return w.rearrange("(k p) n -> p k n", p=P)

        def row_all(v):
            return v.partition_broadcast(P)

        x_v = x.rearrange("b (n p) e -> p (b n) e", p=P)
        o_v = out.rearrange("b (n p) e -> p (b n) e", p=P)

        ld_c = load("c", cst[:, :], const)
        ld_x = [load("x0", xin[:, 0:4, :], x_v[:, 0:4, :])]
        ld_ctx = load("ctx", ctx[:, :, :], ctx_in.rearrange("b t e -> t b e"), act)
        s_rows = sem("ld_rows")
        for r0, n, v in ((0, 2, bq), (2, 2, bk), (4, 2, bv), (6, 8, b1[0, :])):
            act.run(lambda e, r0=r0, n=n, v=v: e.dma_start(
                rows[r0:r0 + n, :], v.rearrange("(k p) -> k p", p=P)).then_inc(s_rows, 16))
        ld_rows = (s_rows, 64)
        ld_wk = load("wk", wk[:, :, :], wview(Wk), act)
        ld_m = load("m", mrow[:, :, :], mask[0, 0].rearrange("(n p) t -> p n t", p=P), act)
        ld_wq = load("wq", wq[:, :, :], wview(Wq))
        ld_wv = load("wv", wv[:, :, :], wview(Wv), act)
        ld_bo = load("bo", bo_r[:, :], row_all(bo))
        ld_wo = load("wo", wo[:, :, :], wview(Wo))
        ld_w1 = load("w1", w1raw.rearrange("p (k n) -> p k n", k=2), wview(w1[0]))
        ld_w2 = load("w2", w2raw.rearrange("p (k n) -> p k n", k=8), wview(w2[0]))
        ld_x.append(load("x1", xin[:, 4:8, :], x_v[:, 4:8, :]))
        ld_b2 = load("b2", b2_r[:, :], row_all(b2[0]))
        ld_ga = load("ga", ga_r[:, :], row_all(gamma))
        ld_be = load("be", be_r[:, :], row_all(beta))
        ld_x.append(load("x2", xin[:, 8:12, :], x_v[:, 8:12, :]))
        ld_x.append(load("x3", xin[:, 12:16, :], x_v[:, 12:16, :]))

        dve.wait(ld_c)
        t_idb = dve.done(lambda e: e.tensor_copy(identb[:, :], ident))
        id77 = cst[0:TK, 0:TK].unsqueeze(1).to_broadcast([TK, 4, TK])
        t_rep = dve.done(lambda e: e.tensor_copy(rep[:, :].rearrange("p (r t) -> p r t", t=TK), id77))
        t_repb = dve.done(lambda e: e.tensor_copy(repb[:, :].rearrange("p (r t) -> p r t", t=TK), id77))
        t_mh = pool.done(lambda e: e.memset(mh[:, :], -0.5))

        def rstd(marks):
            dve.wait(*marks)
            for n in range(4):
                m = dve.done(lambda e, n=n: e.bn_aggr(mv[:, n, :], st[:, n, :]))
            dve.wait(m)
            m = dve.done(lambda e: e.tensor_scalar(ve[:, :], mv[:, :, 1], EPS, None, ALU.add))
            pool.wait(m, t_mh)
            return pool.done(lambda e: e.tensor_tensor(rs[:, :], ve[:, :], mh[:, :], ALU.pow))

        t_xnT = [None] * NC
        t_q = {}
        t_xb = [None] * NC
        t_xn = [None] * NC
        last = {"xn_read": [], "xnT_read": [], "q_read": {}, "Kb_read": {}, "Vb_read": {}, "stat": None, "P_read": {}, "acc_read": [], "aT_read": [],
                "xb_read": {}, "x1_read": {}, "xn2_read": {}, "x2_read": [], "h_read": [], "yb_read": {},
                "ob_read": {}, "xn2b_read": {}, "x1b_read": {}, "PT_read": {}, "hr_read": {}, "S_read": {},
                "rd": {}}

        def norm1(c):
            dve.wait(ld_x[c])
            for n in range(4):
                m = dve.done(lambda e, n=n: e.bn_stats(st[:, n, :], xin[:, 4 * c + n, :]))
            r = rstd([m])
            dve.wait(r, *last["xn_read"])
            for n in range(4):
                m = dve.done(lambda e, n=n: e.tensor_scalar(
                    xn[:, n, :], xin[:, 4 * c + n, :], mv[:, n, 0:1], rs[:, n:n + 1], ALU.subtract, ALU.mult))
            t_xn[c] = m

        def turn1(c):
            pe.wait(t_xn[c], ld_c)
            for k in range(2):
                t = bank.take()
                for n in range(4):
                    f = lambda e, n=n, t=t, k=k: e.transpose(t[:, n * 128:(n + 1) * 128], xn[:, n, k * 128:(k + 1) * 128], ident)
                    m = pe.done(f) if n == 3 else pe.run(f)
                act.wait(m, *last["xnT_read"])
                a = act.done(lambda e, t=t, k=k: e.copy(xnT[:, k, :], t[:, :]))
                bank.give(t, a)
            last["xn_read"] = [m]
            t_xnT[c] = a

        def xbias(c):
            pool.wait(ld_bo, t_xn[c])
            for n in range(4):
                t_xb[c] = pool.done(lambda e, n=n: e.tensor_tensor(xin[:, 4 * c + n, :], xin[:, 4 * c + n, :], bo_r[:, :], ALU.add))

        def qproj(c, g):
            pe.wait(t_xnT[c], ld_wq)
            t = bank.take()
            pe.run(lambda e: e.matmul(t[:, :], wq[:, 0, g * 128:(g + 1) * 128], xnT[:, 0, :], start=True, stop=False))
            m = pe.done(lambda e: e.matmul(t[:, :], wq[:, 1, g * 128:(g + 1) * 128], xnT[:, 1, :], start=False, stop=True))
            act.wait(m, t_cols, *last["q_read"].get(g, []))
            a = act.done(lambda e: e.activation(qh[:, g, :], t[:, :], ACT.Identity, bias=cols[:, g:g + 1]))
            dve.wait(a)
            d = dve.done(lambda e: e.scalar_tensor_tensor(ql[:, g, :], t[:, :], cols[:, g:g + 1], qh[:, g, :].bitcast(F32),
                                                          ALU.add, ALU.subtract))
            bank.give(t, d)
            last["xnT_read"] = [m]
            t_q[c, g] = d

        pe.wait(ld_rows, ld_c)
        t = bank.take()
        m = pe.done(lambda e, t=t: e.transpose(t[:, 0:14], rows[:, :], cst[0:14, 0:14]))
        dve.wait(m)
        t_cols = dve.done(lambda e, t=t: e.tensor_copy(cols[:, :], t[:, 0:14]))
        bank.give(t, t_cols)
        dve.wait(t_cols)
        t_bk4 = dve.done(lambda e: e.tensor_scalar(bk4[:, :], cols[:, 2:4], 0.25, None, ALU.mult))

        norm1(0)
        turn1(0)
        qproj(0, 0)
        qproj(0, 1)
        xbias(0)

        pe.wait(ld_ctx)
        t = bank.take()
        for bb in range(2):
            for k in range(2):
                m = pe.done(lambda e, t=t, bb=bb, k=k: e.transpose(
                    t[:, (2 * k + bb) * TK:(2 * k + bb + 1) * TK], ctx[:, bb, k * 128:(k + 1) * 128], cst[0:TK, 0:TK]))
        act.wait(m)
        t_ctxT = act.done(lambda e, t=t: e.copy(ctxT[:, :, :, :].rearrange("p k b t -> p (k b t)"), t[:, 0:4 * TK]))
        bank.give(t, t_ctxT)
        pe.wait(t_ctxT, ld_wk)
        for g in range(2):
            t = bank.take()
            for k in range(2):
                f = lambda e, t=t, g=g, k=k: e.matmul(
                    t[:, 0:2 * TK], wk[:, k, g * 128:(g + 1) * 128], ctxT[:, k, :, :].rearrange("p b t -> p (b t)"),
                    start=(k == 0), stop=(k == 1))
                m = pe.done(f) if k else pe.run(f)
            act.wait(m, t_bk4)
            a = act.done(lambda e, t=t, g=g: e.activation(kraw[:, g, :], t[:, 0:2 * TK], ACT.Identity, bias=bk4[:, g:g + 1], scale=0.25))
            bank.give(t, a)
            dve.wait(a)
            kr = kraw[:, g, :].rearrange("p (b t) -> p b t", b=2)
            d = dve.done(lambda e, g=g, kr=kr: e.tensor_copy(kT[:, g, :, 0, :], kr))
            dve.wait(d)
            t_kT = dve.done(lambda e, g=g, kr=kr: e.tensor_tensor(kT[:, g, :, 1, :], kr, kT[:, g, :, 0, :].bitcast(F32), ALU.subtract))

        t_Kb = {}

        def keys(bb, g):
            dve.wait(t_kT, *last["Kb_read"].get(g, []))
            for hl_ in range(2):
                t_Kb[bb, g] = dve.done(lambda e, hl_=hl_: e.tensor_tensor(
                    Kb[:, g, hl_, :].rearrange("p (h t) -> p h t", t=TK),
                    kT[:, g, bb, hl_, :].bitcast(F32).unsqueeze(1).to_broadcast([P, 8, TK]),
                    bmask.unsqueeze(2).to_broadcast([P, 8, TK]), ALU.mult))

        keys(0, 0)
        dve.wait(ld_m)
        m = dve.done(lambda e: e.tensor_scalar(crow[:, :, :], mrow[:, :, :], 1.0, BIG, ALU.subtract, ALU.mult))
        pe.wait(m, t_idb)
        t = bank.take()
        tb = t[:, :].bitcast(BF16)
        for n in range(8):
            f = lambda e, tb=tb, n=n: e.transpose(tb[0:TK, n * 128:(n + 1) * 128], crow[:, n, :], identb[:, :])
            m = pe.done(f) if n == 7 else pe.run(f)
        dve.wait(m)
        t_cT = dve.done(lambda e, tb=tb: e.tensor_copy(cT[:, :], tb[0:TK, :]))
        bank.give(t, t_cT)

        def values():
            pe.wait(t_ctxT, ld_wv)
            marks = []
            for bb in range(2):
                t = bank.take()
                for k in range(2):
                    f = lambda e, t=t, bb=bb, k=k: e.matmul(t[0:TK, 0:E], ctxT[:, k, bb, :], wv[:, k, :], start=(k == 0), stop=(k == 1))
                    m = pe.done(f) if k else pe.run(f)
                act.wait(m)
                a = act.done(lambda e, t=t, bb=bb: e.copy(vsb[:, bb, :], t[0:TK, 0:E]))
                bank.give(t, a)
                marks.append(a)
            for bb in range(2):
                for j in range(5):
                    pe.wait(marks[bb], t_rep)
                    t = bank.take()
                    o = 128 * j % TK
                    m = pe.done(lambda e, t=t, bb=bb, o=o: e.matmul(t[:, 0:E], rep[:, o:o + 128], vsb[:, bb, :], start=True, stop=True))
                    dve.wait(m)
                    a = dve.done(lambda e, t=t, bb=bb, j=j: e.tensor_tensor(
                        Vb[:, bb, j, :].rearrange("p (g h d) -> p g h d", g=2, d=D),
                        t[:, 0:E].rearrange("p (g h d) -> p g h d", g=2, d=D),
                        vmask[:, 8 * j:8 * j + 8].unsqueeze(1).unsqueeze(3).to_broadcast([P, 2, 8, D]), ALU.mult))
                    bank.give(t, a)
            return a

        t_w1, t_w2 = [], []

        def split(raw, hi, lo, loaded, marks, a, b):
            act.wait(loaded)
            m = act.done(lambda e: e.copy(hi[:, a:b], raw[:, a:b]))
            pool.wait(m)
            marks.append(pool.done(lambda e: e.tensor_tensor(lo[:, a:b], raw[:, a:b], hi[:, a:b].bitcast(F32), ALU.subtract)))

        t_P = {}
        units = [0]

        def scores(i, g):
            c, n, bb = i // 4, i % 4, i // 8
            u = units[0] % 2
            units[0] += 1
            s = S[u]
            pe.wait(t_q[c, g], t_Kb[bb, g], t_cT, t_repb, *last["S_read"].get(u, []))
            for y, w in ((qh, 0), (qh, 1), (ql, 0)):
                for h in range(2):
                    pe.run(lambda e, h=h, y=y, w=w: e.matmul(
                        s[:, h, 0:4 * TK], y[:, g, n * 128:(n + 1) * 128],
                        Kb[:, g, w, h * 4 * TK:(h + 1) * 4 * TK], start=(y is qh and w == 0), stop=False))
            q0 = (i % 8) * 128
            for h in range(2):
                f = lambda e, h=h: e.matmul(s[:, h, 0:4 * TK], cT[:, q0:q0 + 128], repb[:, :], start=False, stop=True)
                m = pe.done(f) if h else pe.run(f)
            last["q_read"][g] = [m]
            last["Kb_read"][g] = [m]
            sv = s[:, :, 0:4 * TK].rearrange("p b (h t) -> p b h t", t=TK)
            pm = Pm[:, n, g, :]
            p3 = pm.rearrange("p (h t) -> p h t", t=TK)
            dve.wait(m)
            m = dve.done(lambda e: e.tensor_reduce(mx[:, u, :].rearrange("p (b h) -> p b h", b=2), sv, AX_X, ALU.max))
            dve.wait(m, *last["P_read"].get(g, []))
            m = dve.done(lambda e: e.tensor_tensor(
                pm.rearrange("p (b h t) -> p b h t", b=2, t=TK), sv,
                mx[:, u, :].rearrange("p (b h) -> p b h", b=2).unsqueeze(3).to_broadcast([P, 2, 4, TK]), ALU.subtract))
            last["S_read"][u] = [m]
            act.wait(m)
            a = act.done(lambda e: e.activation(pm, pm, ACT.Exp))

            def rest():
                dve.wait(a)
                m = dve.done(lambda e: e.tensor_reduce(dn[:, u, :], p3, AX_X, ALU.add))
                dve.wait(m, *last["rd"].get(u, []))
                m = dve.done(lambda e: e.reciprocal(rd[:, u, :], dn[:, u, :]))
                pool.wait(m)
                t_P[i, g] = pool.done(lambda e: e.tensor_tensor(p3, p3, rd[:, u, :].unsqueeze(2).to_broadcast([P, 8, TK]), ALU.mult))
                last["rd"][u] = [t_P[i, g]]
            return rest

        t_aT = {}
        pts = [0]
        pend = []

        def pv():
            bb, g, j, slot, a = pend.pop(0)
            pe.wait(a, t_Vb, *(last["acc_read"] if j == 0 else []))
            r = KROWS[j]
            m = pe.done(lambda e: e.matmul(acc[:, :], Vb[0:r, bb, j, g * 128:(g + 1) * 128], PT[0:r, slot, :],
                                           start=(j == 0), stop=(j == 4)))
            last["PT_read"][slot] = [m]
            return m

        def weigh(c, g, j):
            r = KROWS[j]
            t = bank.take()
            for n in range(4):
                pe.wait(t_P[4 * c + n, g])
                f = lambda e, n=n, t=t, r=r, j=j, g=g: e.transpose(t[0:r, n * 128:(n + 1) * 128], Pm[:, n, g, j * 128:j * 128 + r], ident)
                m = pe.done(f) if n == 3 else pe.run(f)
            slot = pts[0] % 4
            pts[0] += 1
            act.wait(m, *last["PT_read"].get(slot, []))
            a = act.done(lambda e, t=t, r=r, slot=slot: e.copy(PT[0:r, slot, :], t[0:r, :]))
            bank.give(t, a)
            pend.append((c // 2, g, j, slot, a))
            if j == 4:
                last["P_read"][g] = [m]

        def weigh_end(c, g):
            m = pv()
            act.wait(m, *last["aT_read"])
            a = act.done(lambda e: e.activation(aT[:, g, :], acc[:, :], ACT.Identity, bias=cols[:, 4 + g:5 + g]))
            last["acc_read"] = [a]
            t_aT[c] = a

        t_x2 = {}
        t_n2 = {}
        t_x2T = {}

        def out_norm2(c):
            pe.wait(t_aT[c], ld_wo)
            for h in range(2):
                t = bank.take()
                for n in range(2):
                    q = (2 * h + n) * 128
                    for k in range(2):
                        f = lambda e, t=t, n=n, q=q, k=k: e.matmul(t[:, n * E:(n + 1) * E], aT[:, k, q:q + 128], wo[:, k, :],
                                                                   start=(k == 0), stop=(k == 1))
                        m = pe.done(f) if n and k else pe.run(f)
                dve.wait(m, t_xb[c], *t_w2, *last["x1_read"].get(c % 2, []))
                d = dve.done(lambda e, t=t, h=h: e.tensor_tensor(
                    x1[:, c % 2, 2 * h:2 * h + 2, :].rearrange("p n e -> p (n e)"), t[:, :],
                    xin[:, 4 * c + 2 * h:4 * c + 2 * h + 2, :].rearrange("p n e -> p (n e)"), ALU.add))
                bank.give(t, d)
                dve.wait(d)
                for n in range(2):
                    s = dve.done(lambda e, h=h, n=n: e.bn_stats(st[:, 2 * h + n, :], x1[:, c % 2, 2 * h + n, :]))
            last["aT_read"] = [m]
            r = rstd([s])
            dve.wait(r, *t_w1, *last["xn2_read"].get(c % 2, []))
            for n in range(4):
                m = dve.done(lambda e, n=n: e.tensor_scalar(xn2[:, c % 2, n, :], x1[:, c % 2, n, :], mv[:, n, 0:1], rs[:, n:n + 1], ALU.subtract, ALU.mult))
            t_n2[c] = m

        def turn2(c):
            pe.wait(t_n2[c])
            for k in range(2):
                t = bank.take()
                for n in range(4):
                    f = lambda e, n=n, t=t, k=k: e.transpose(t[:, n * 128:(n + 1) * 128], xn2[:, c % 2, n, k * 128:(k + 1) * 128], ident)
                    m = pe.done(f) if n == 3 else pe.run(f)
                act.wait(m, *last["x2_read"])
                a = act.done(lambda e, t=t, k=k: e.copy(x2h[:, k, :], t[:, :]))
                dve.wait(a)
                d = dve.done(lambda e, t=t, k=k: e.tensor_tensor(x2l[:, k, :], t[:, :], x2h[:, k, :].bitcast(F32), ALU.subtract))
                bank.give(t, d)
            t_x2[c] = d
            t_x2T[c] = [m]

        def biases2(c):
            pool.wait(*t_x2T[c], ld_b2, ld_be)
            for n in range(4):
                pool.run(lambda e, n=n: e.tensor_tensor(xn2[:, c % 2, n, :], xn2[:, c % 2, n, :], b2_r[:, :], ALU.add))
                p = pool.done(lambda e, n=n: e.tensor_tensor(x1[:, c % 2, n, :], x1[:, c % 2, n, :], be_r[:, :], ALU.add))
            t_x1b[c] = p

        t_x1b = {}
        t_h = {}

        def ffn1(c, f_):
            pe.wait(t_x2[c], *t_w1)
            t = bank.take()
            n = 0
            for k in range(2):
                o = k * F + f_ * 128
                for w, y in ((w1h, x2h), (w1h, x2l), (w1l, x2h)):
                    f = lambda e, w=w, y=y, n=n, o=o, k=k, t=t: e.matmul(t[:, :], w[:, o:o + 128], y[:, k, :], start=(n == 0), stop=(n == 5))
                    m = pe.done(f) if n == 5 else pe.run(f)
                    n += 1
            if f_ == 7:
                last["x2_read"] = [m]
            r = f_ % 2
            act.wait(m, *last["hr_read"].get(r, []))
            a = act.done(lambda e, t=t, r=r: e.activation(hr[:, r, :], t[:, :], ACT.Relu, bias=cols[:, 6 + f_:7 + f_]))
            bank.give(t, a)
            act.wait(a, *last["h_read"])
            d = act.done(lambda e, r=r: e.copy(hh[:, f_, :], hr[:, r, :]))
            eng = pool if f_ % 2 and c < NC - 1 else dve
            eng.wait(d)
            d = eng.done(lambda e, r=r: e.tensor_tensor(hl[:, f_, :], hr[:, r, :], hh[:, f_, :].bitcast(F32), ALU.subtract))
            last["hr_read"][r] = [d]
            t_h.setdefault(c, []).append(d)

        s_out = [sem("stored0"), sem("stored1")]
        stores = [0, 0]

        open2 = {}

        def ffn2(c, h, part):
            pe.wait(*t_h[c], *t_w2)
            if part == 0:
                open2[h] = bank.take()
            t = open2[h]
            n = part // 2
            q = (2 * h + n) * 128
            cnt = 12 * (part % 2)
            for f_ in range(4 * (part % 2), 4 * (part % 2) + 4):
                for y, w in ((hh, w2h), (hh, w2l), (hl, w2h)):
                    f = lambda e, y=y, w=w, f_=f_, q=q, n=n, cnt=cnt, t=t: e.matmul(
                        t[:, n * E:(n + 1) * E], y[:, f_, q:q + 128], w[:, f_ * E:(f_ + 1) * E], start=(cnt == 0), stop=(cnt == 23))
                    m = pe.done(f) if n and cnt == 23 else pe.run(f)
                    cnt += 1
            if part < 3:
                return
            if h == 1:
                last["h_read"] = [m]
            u = h

            def rest():
                dve.wait(m, t_x1b[c], *last["ob_read"].get(u, []))
                d = dve.done(lambda e: e.tensor_tensor(
                    yb[:, u, :, :].rearrange("p n e -> p (n e)"), t[:, :],
                    xn2[:, c % 2, 2 * h:2 * h + 2, :].rearrange("p n e -> p (n e)"), ALU.add))
                bank.give(t, d)
                last["xn2_read"][c % 2] = [d]
                dve.wait(d)
                for n in range(2):
                    s = dve.done(lambda e, n=n: e.bn_stats(st[:, n, :], yb[:, u, n, :]))
                dve.wait(s)
                for n in range(2):
                    s = dve.done(lambda e, n=n: e.bn_aggr(mv[:, n, :], st[:, n, :]))
                dve.wait(s)
                s = dve.done(lambda e: e.tensor_scalar(ve[:, 0:2], mv[:, 0:2, 1], EPS, None, ALU.add))
                pool.wait(s, t_mh)
                s = pool.done(lambda e: e.tensor_tensor(rs[:, 0:2], ve[:, 0:2], mh[:, 0:2], ALU.pow))
                dve.wait(s)
                for n in range(2):
                    s = dve.done(lambda e, n=n: e.tensor_scalar(yb[:, u, n, :], yb[:, u, n, :], mv[:, n, 0:1], rs[:, n:n + 1], ALU.subtract, ALU.mult))
                dve.wait(s, ld_ga)
                gb = ga_r[:, :].unsqueeze(1).to_broadcast([P, 2, E])
                s = dve.done(lambda e: e.tensor_tensor(yb[:, u, :, :], yb[:, u, :, :], gb, ALU.mult))
                dve.wait(s)
                s = dve.done(lambda e: e.tensor_tensor(yb[:, u, :, :], yb[:, u, :, :], x1[:, c % 2, 2 * h:2 * h + 2, :], ALU.add))
                last["x1_read"][c % 2] = [s]
                sp.wait(s)
                n0 = 4 * c + 2 * h
                sp.run(lambda e: e.dma_start(o_v[:, n0:n0 + 2, :], yb[:, u, :, :]).then_inc(s_out[u], 16))
                stores[u] += 1
                last["ob_read"][u] = [(s_out[u], 16 * stores[u])]
            rest()

        pending = []

        def score_piece(c, n, g):
            r = scores(4 * c + n, g)
            if pending:
                pending.pop()()
            pending.append(r)

        def flush():
            if pending:
                pending.pop()()

        def weave(*plans):
            pieces = [(at, k, what) for k, plan in enumerate(plans) for at, what in plan]
            for _, _, what in sorted(pieces, key=lambda p: (p[0], p[1])):
                what()

        def spread(a, b, whats):
            return [(a + (b - a) * k / len(whats), w) for k, w in enumerate(whats)]

        def later(f, *args):
            return lambda: f(*args)

        def score_plan(b, c, g):
            return spread(0, b, [later(score_piece, c, n, g) for n in range(4)])

        def weigh_plan(a, b, lag, c, g):
            step = (b - a) / 5
            return ([(a, flush)] + [(a + step * j, later(weigh, c, g, j)) for j in range(5)]
                    + [(a + step * (j + lag), pv) for j in range(4)] + [(a + step * (4 + lag), later(weigh_end, c, g))])

        def ffn1_plan(a, b, c):
            return spread(a, b, [later(ffn1, c, f_) for f_ in range(8)])

        def ffn2_plan(a, b, c):
            return spread(a, b, [later(ffn2, c, h, part) for h in range(2) for part in range(4)])

        def split_plan(a, b):
            return spread(a, b, [later(split, *w, 512 * k, 512 * k + 512) for w in (
                (w1raw, w1h, w1l, ld_w1, t_w1), (w2raw, w2h, w2l, ld_w2, t_w2)) for k in range(4)])

        for n in range(4):
            score_piece(0, n, 0)
        t_Vb = values()
        keys(0, 1)
        norm1(1)
        for c in range(NC + 1):
            if c:
                plans = [weigh_plan(A[0], A[1], A[7], c - 1, 1), [(A[2], later(out_norm2, c - 1)), (A[3], later(turn2, c - 1))]]
                if c < NC:
                    plans.append(score_plan(A[8], c, 0))
                    plans.append([(0.0, later(qproj, c, 1))])
                if c > 1:
                    plans.append(ffn2_plan(A[4], A[5], c - 2))
                if c == NC:
                    plans.append([(0.99, later(biases2, c - 1))])
                if c == 2:
                    plans.append([(0.0, later(keys, 1, 1))])
                weave(*plans)
            if c < NC:
                plans = [score_plan(B[9], c, 1), weigh_plan(B[0], B[1], B[8], c, 0)]
                if c == 1:
                    plans.append([(0.9, later(keys, 1, 0))])
                if c == 0:
                    plans.append(split_plan(0.05, 0.95))
                if c:
                    plans.append(ffn1_plan(B[2], B[3], c - 1))
                    plans.append([(B[4], later(biases2, c - 1))])
                if c + 1 < NC:
                    if c + 2 < NC:
                        plans.append([(A[6], later(norm1, c + 2))])
                    plans.append([(B[5], later(turn1, c + 1)), (B[6], later(qproj, c + 1, 0)), (B[7], later(xbias, c + 1))])
                weave(*plans)
        for f_ in range(8):
            ffn1(NC - 1, f_)
        for h in range(2):
            for part in range(4):
                ffn2(NC - 1, h, part)
        sp.wait(*((s_out[u], 16 * stores[u]) for u in range(2)))

        block = stack.enter_context(nc.Block())
        block.sync(sp.play)
        block.scalar(act.play)
        block.vector(dve.play)
        block.gpsimd(pool.play)
        block.tensor(pe.play)


_INS = ["x", "ctx_1024", "mask_1x1xSxS2_fk0", "L0_xattn_Wq", "L0_xattn_bq", "L0_xattn_Wk", "L0_xattn_bk",
        "L0_xattn_Wv", "L0_xattn_bv", "L0_xattn_Wo", "L0_xattn_bo", "L0_ffn_w1", "L0_ffn_b1", "L0_ffn_w2",
        "L0_ffn_b2", "L0_ffn_gamma", "L0_ffn_beta"]


def _constants():
    c = np.zeros((128, 176), np.float32)
    p = np.arange(128)
    c[p, p] = 1.0
    c[p, 128 + p // 16] = 1.0
    for j in range(5):
        h = (128 * j + p) // 77
        ok = h < 8
        c[p[ok], 136 + 8 * j + h[ok]] = 1.0
    return c


def kernel(**inputs):
    import numpy as _np
    import concourse.bacc as _bacc
    from concourse import mybir as _mybir
    from concourse.bass_utils import run_bass_kernel_spmd as _run

    nc = _bacc.Bacc("TRN2", target_bir_lowering=False, num_devices=1)
    arrays, args = {}, []
    for name in _INS + ["const"]:
        a = _constants() if name == "const" else _np.ascontiguousarray(inputs[name])
        arrays[f"in_{name}_dram"] = a
        args.append(nc.dram_tensor(f"in_{name}_dram", a.shape, _mybir.dt.from_np(a.dtype), kind="ExternalInput").ap())
    out = nc.dram_tensor("out_0_dram", (2, 1024, 256), F32, kind="ExternalOutput").ap()
    build(nc, *args, out)
    r = _run(nc, [arrays], core_ids=[0])
    return r.results[0]["out_0_dram"]
```

```python
from contextlib import ExitStack

import numpy as np
import concourse.bass as bass
from concourse import mybir

F32 = mybir.dt.float32
F32R = mybir.dt.float32r
BF16 = mybir.dt.bfloat16
ALU = mybir.AluOpType
ACT = mybir.ActivationFunctionType
AX_X = mybir.AxisListType.X

P = 128
E = 256
NT = 16
NC = 4
H = 16
D = 16
TK = 77
F = 1024
G = 8 * TK
A = [0.176, 0.437, 0.5, 0.76, 0.143, 0.823, 0.751, 1.605, 0.902, 0.073, 0.176, 0.4, 0.5, 0.581, 0, 1.0, 0.636, 1.787, 0.909, 0.106]
C = [0.331, 1.174, 0.85, 0.963, 0.515, 1.105, 0.655]
LAGS = [3, 2, 1, 2]
EPS = 1e-5
BIG = float(2.0 ** 60)
KROWS = [128, 128, 128, 128, G - 512]
B = [0.311, 1.393, 0, 1.611, 0.371, 0.143, 0.609, 1.146, 1.501, 0.743, 0.219, 1.556, 0, 0.744, 1.171, 0.189, 0.617, 0.744, 1.564, 0.743]



class Engine:

    def __init__(self, sem):
        self.sem, self.count, self.queue, self.seen = sem, 0, [], {}

    def wait(self, *marks):
        for sem, value in marks:
            if self.seen.get(sem.name, 0) < value:
                self.seen[sem.name] = value
                self.queue.append(lambda e, sem=sem, value=value: e.wait_ge(sem, value))

    def run(self, what):
        self.queue.append(what)

    def done(self, what):
        self.count += 1
        self.queue.append(lambda e: what(e).then_inc(self.sem, 1))
        return (self.sem, self.count)

    def play(self, e):
        for what in self.queue:
            what(e)


class Banks:

    def __init__(self, pe, tensors):
        self.pe, self.idle = pe, [(t, None) for t in tensors]

    def take(self):
        t, reader = self.idle.pop(0)
        if reader is not None:
            self.pe.wait(reader)
        return t

    def give(self, t, reader):
        self.idle.append((t, reader))


def build(nc, x, ctx_in, mask, Wq, bq, Wk, bk, Wv, bv, Wo, bo, w1, b1, w2, b2, gamma, beta, const, out):
    stack = ExitStack()
    with stack:
        def sb(name, shape, dt=F32):
            return stack.enter_context(nc.sbuf_tensor(name, shape, dt))

        def ps(name, shape, dt=F32):
            return stack.enter_context(nc.psum_tensor(name, shape, dt))

        def sem(name):
            return stack.enter_context(nc.semaphore(name))

        cst = sb("cst", [P, 172])
        ident = cst[:, 0:128]
        bmask = cst[:, 128:132]
        vmask = cst[:, 132:172]
        rep = sb("rep", [TK, 4 * TK])
        repb = sb("repb", [TK, 4 * TK], BF16)
        identb = sb("identb", [P, P], BF16)
        hr = sb("hr", [P, 2, 512])
        yb = sb("yb", [P, 2, 2, E])
        hr_all = hr[:, :, :].rearrange("p a n -> p (a n)")
        mrow = hr_all[:, 0:8 * TK].rearrange("p (n t) -> p n t", t=TK)
        kraw = yb[:, 1, :, :].rearrange("p a n -> p (a n)")[:, 0:4 * TK].rearrange("p (r n) -> p r n", r=2)
        ctx = yb[0:TK, 0, :, :]
        cT = sb("cT", [TK, 1024], BF16)
        rows = sb("rows", [16, P])
        cols = sb("cols", [P, 16])
        bk4 = sb("bk4", [P, 4])
        bo_r = sb("bo_r", [P, E])
        b2_r = sb("b2_r", [P, E])
        ga_r = sb("ga_r", [P, E])
        be_r = sb("be_r", [P, E])
        wq = sb("wq", [P, 2, E])
        kT = sb("kT", [P, 4, 2, 2, TK], F32R)
        vsb = sb("vsb", [TK, 2, E])
        Kb = sb("Kb", [P, 4, 2, 4 * TK], F32R)
        Vb = sb("Vb", [P, 2, 5, E])
        w1h = sb("w1h", [P, 2048], F32R)
        w1l = sb("w1l", [P, 2048], F32R)
        w2h = sb("w2h", [P, 2048], F32R)
        w2l = sb("w2l", [P, 2048], F32R)
        xin = sb("xin", [P, NT, E])
        xn = sb("xn", [P, 4, E])
        xnT = sb("xnT", [P, 2, 512])
        qs = sb("qs", [P, 4, 512], F32R)
        Pm = sb("Pm", [P, 4, 2, G])
        PT = sb("PT", [P, 4, 512])
        aT = sb("aT", [P, 2, 512], F32R)
        x1 = sb("x1", [P, 2, 4, E])
        xn2 = sb("xn2", [P, 2, 4, E])
        w1raw = xn2[:, :, :, :].rearrange("p a n e -> p (a n e)")
        w2raw = x1[:, :, :, :].rearrange("p a n e -> p (a n e)")
        x2h = sb("x2h", [P, 2, 512], F32R)
        x2l = sb("x2l", [P, 2, 512], F32R)
        hh = sb("hh", [P, 8, 512], F32R)
        hl = sb("hl", [P, 8, 512], F32R)
        mx = sb("mx", [P, 2, 8])
        dn = sb("dn", [P, 2, 8])
        rd = sb("rd", [P, 2, 8])
        stats = [(sb(f"st{i}", [P, n, 6]), sb(f"mv{i}", [P, n, 2]), sb(f"ve{i}", [P, n]), sb(f"rs{i}", [P, n]))
                 for i, n in enumerate((4, 4, 2, 2))]
        mh = sb("mh", [P, 4])

        with ExitStack() as setup:
            def early(name, shape, dt=F32):
                return setup.enter_context(nc.sbuf_tensor(name, list(shape), dt))

            wk = early("wk", [P, 2, E])
            wv = early("wv", [P, 2, E])
            wo = early("wo", [P, 2, E])
            ctxT = early("ctxT", [P, 2, 2, TK])
            crow = early("crow", [P, 8, TK], BF16)
        aTl = sb("aTl", [P, 2, 512], F32R)
        wol = sb("wol", [P, 2, E], F32R)
        woh = sb("woh", [P, 2, E], F32R)

        S = [ps("S0", [P, 2, 512]), ps("S1", [P, 2, 512])]
        W = [ps(f"W{i}", [P, 512]) for i in range(4)]

        pe = Engine(sem("pe_done"))
        dve = Engine(sem("dve_done"))
        act = Engine(sem("act_done"))
        pool = Engine(sem("pool_done"))
        sp = Engine(sem("sp_done"))
        bank = Banks(pe, W[0:3])
        acc = W[3]

        def load(name, dst, src, eng=sp):
            s = sem("ld_" + name)
            eng.run(lambda e: e.dma_start(dst, src).then_inc(s, 16))
            return (s, 16)

        def wview(w):
            return w.rearrange("(k p) n -> p k n", p=P)

        def row_all(v):
            return v.partition_broadcast(P)

        x_v = x.rearrange("b (n p) e -> p (b n) e", p=P)
        o_v = out.rearrange("b (n p) e -> p (b n) e", p=P)

        ld_x = [load("x0", xin[:, 0:4, :], x_v[:, 0:4, :])]
        ld_c = load("c", cst[:, :], const)
        ld_ctx = load("ctx", ctx[:, :, :], ctx_in.rearrange("b t e -> t b e"), act)
        s_rows = sem("ld_rows")
        for r0, n, v in ((0, 2, bq), (6, 2, bv), (8, 8, b1[0, :])):
            act.run(lambda e, r0=r0, n=n, v=v: e.dma_start(
                rows[r0:r0 + n, :], v.rearrange("(k p) -> k p", p=P)).then_inc(s_rows, 16))
        for side in range(2):
            act.run(lambda e, side=side: e.dma_start(
                rows[2:6, 64 * side:64 * side + 64], bk.rearrange("(k p) -> k p", p=64)).then_inc(s_rows, 16))
        ld_rows = (s_rows, 80)
        ld_wk = load("wk", wk[:, :, :], wview(Wk), act)
        ld_m = load("m", mrow[:, :, :], mask[0, 0].rearrange("(n p) t -> p n t", p=P), act)
        ld_wq = load("wq", wq[:, :, :], wview(Wq))
        ld_wv = load("wv", wv[:, :, :], wview(Wv), act)
        ld_bo = load("bo", bo_r[:, :], row_all(bo))
        ld_wo = load("wo", wo[:, :, :], wview(Wo))
        sp.wait(ld_m)
        ld_w1 = load("w1", w1raw.rearrange("p (k n) -> p k n", k=2), wview(w1[0]))
        ld_w2 = load("w2", w2raw.rearrange("p (k n) -> p k n", k=8), wview(w2[0]))
        ld_x.append(load("x1", xin[:, 4:8, :], x_v[:, 4:8, :]))
        ld_b2 = load("b2", b2_r[:, :], row_all(b2[0]))
        ld_ga = load("ga", ga_r[:, :], row_all(gamma))
        ld_be = load("be", be_r[:, :], row_all(beta))
        ld_x.append(load("x2", xin[:, 8:12, :], x_v[:, 8:12, :]))
        ld_x.append(load("x3", xin[:, 12:16, :], x_v[:, 12:16, :]))

        dve.wait(ld_c)
        t_idb = dve.done(lambda e: e.tensor_copy(identb[:, :], ident))
        id77 = cst[0:TK, 0:TK].unsqueeze(1).to_broadcast([TK, 4, TK])
        t_rep = dve.done(lambda e: e.tensor_copy(rep[:, :].rearrange("p (r t) -> p r t", t=TK), id77))
        t_repb = dve.done(lambda e: e.tensor_copy(repb[:, :].rearrange("p (r t) -> p r t", t=TK), id77))
        t_mh = pool.done(lambda e: e.memset(mh[:, :], -0.5))

        steps = []
        clock = [0]

        def after(n, what):
            steps.append((clock[0] + n, what))

        def tick():
            clock[0] += 1
            due = [x for x in steps if x[0] <= clock[0]]
            steps[:] = [x for x in steps if x[0] > clock[0]]
            for _, what in due:
                what()

        def drain():
            while steps:
                tick()

        def rstd(k, mark, na=0, nb=None):
            st, mv, ve, rs = stats[k]
            nb = nb or rs.shape[1]
            dve.wait(mark)
            for n in range(na, nb):
                m = dve.done(lambda e, n=n: e.bn_aggr(mv[:, n, :], st[:, n, :]))
            dve.wait(m)
            m = dve.done(lambda e: e.tensor_scalar(ve[:, na:nb], mv[:, na:nb, 1], EPS, None, ALU.add))
            pool.wait(m, t_mh)
            return pool.done(lambda e: e.tensor_tensor(rs[:, na:nb], ve[:, na:nb], mh[:, na:nb], ALU.pow))

        t_xnT = [None] * NC
        t_q = {}
        t_xb = [None] * NC
        t_xn = [None] * NC
        last = {"xn_read": [], "xnT_read": [], "q_read": {}, "Kb_read": {}, "Vb_read": {}, "stat": None, "P_read": {}, "acc_read": [], "aT_read": [],
                "xb_read": {}, "x1_read": {}, "xn2_read": {}, "x2_read": [], "h_read": [], "yb_read": {},
                "ob_read": {}, "xn2b_read": {}, "x1b_read": {}, "PT_read": {}, "hr_read": {}, "S_read": {},
                "rd": {}}

        def norm1(c):
            st, mv, ve, rs = stats[0]
            dve.wait(ld_x[c])
            for n in range(4):
                m = dve.done(lambda e, n=n: e.bn_stats(st[:, n, :], xin[:, 4 * c + n, :]))
            r = rstd(0, m)

            def scale():
                assert c < 2 or t_xnT[c - 1]
                dve.wait(r, *last["xn_read"])
                for n in range(4):
                    m = dve.done(lambda e, n=n: e.tensor_scalar(
                        xn[:, n, :], xin[:, 4 * c + n, :], mv[:, n, 0:1], rs[:, n:n + 1], ALU.subtract, ALU.mult))
                t_xn[c] = m
            after(LAGS[3], scale)

        def turn1(c):
            pe.wait(t_xn[c], ld_c)
            for k in range(2):
                t = bank.take()
                for n in range(4):
                    f = lambda e, n=n, t=t, k=k: e.transpose(t[:, n * 128:(n + 1) * 128], xn[:, n, k * 128:(k + 1) * 128], ident)
                    m = pe.done(f) if n == 3 else pe.run(f)
                act.wait(m, *last["xnT_read"])
                a = act.done(lambda e, t=t, k=k: e.copy(xnT[:, k, :], t[:, :]))
                bank.give(t, a)
            last["xn_read"] = [m]
            t_xnT[c] = a

        def xbias(c):
            pool.wait(ld_bo, t_xn[c])
            for n in range(0, 4, 2):
                xx = xin[:, 4 * c + n:4 * c + n + 2, :]
                t_xb[c] = pool.done(lambda e, xx=xx: e.tensor_tensor(xx, xx, bo_r[:, :].unsqueeze(1).to_broadcast([P, 2, E]), ALU.add))

        def qproj(c, g):
            pe.wait(t_xnT[c], ld_wq)
            t = bank.take()
            pe.run(lambda e: e.matmul(t[:, :], wq[:, 0, g * 128:(g + 1) * 128], xnT[:, 0, :], start=True, stop=False))
            m = pe.done(lambda e: e.matmul(t[:, :], wq[:, 1, g * 128:(g + 1) * 128], xnT[:, 1, :], start=False, stop=True))
            act.wait(m, t_cols, *last["q_read"].get(g, []))
            halves = [(slice(64 * s_, 64 * s_ + 64), slice(64 - 64 * s_, 128 - 64 * s_), 2 * g + s_) for s_ in range(2)]
            for hi, lo, k in halves:
                a = act.done(lambda e, hi=hi, k=k: e.activation(qs[hi, k, :], t[hi, :], ACT.Identity, bias=cols[hi, g:g + 1]))
            dve.wait(a)
            for hi, lo, k in halves:
                d = dve.done(lambda e, hi=hi, lo=lo, k=k: e.scalar_tensor_tensor(
                    qs[lo, k, :], t[hi, :], cols[hi, g:g + 1], qs[hi, k, :].bitcast(F32), ALU.add, ALU.subtract))
            bank.give(t, d)
            last["xnT_read"] = [m]
            t_q[c, g] = d

        pe.wait(ld_rows, ld_c)
        t = bank.take()
        m = pe.done(lambda e, t=t: e.transpose(t[:, 0:16], rows[:, :], cst[0:16, 0:16]))
        dve.wait(m)
        t_cols = dve.done(lambda e, t=t: e.tensor_copy(cols[:, :], t[:, 0:16]))
        bank.give(t, t_cols)
        dve.wait(t_cols)
        t_bk4 = dve.done(lambda e: e.tensor_scalar(bk4[:, :], cols[:, 2:6], 0.25, None, ALU.mult))

        norm1(0)
        drain()
        turn1(0)
        pe.wait(ld_ctx)
        t = bank.take()
        for bb in range(2):
            for k in range(2):
                m = pe.done(lambda e, t=t, bb=bb, k=k: e.transpose(
                    t[:, (2 * k + bb) * TK:(2 * k + bb + 1) * TK], ctx[:, bb, k * 128:(k + 1) * 128], cst[0:TK, 0:TK]))
        act.wait(m)
        t_ctxT = act.done(lambda e, t=t: e.copy(ctxT[:, :, :, :].rearrange("p k b t -> p (k b t)"), t[:, 0:4 * TK]))
        bank.give(t, t_ctxT)
        dve.wait(ld_m)
        t_crow = dve.done(lambda e: e.tensor_scalar(crow[:, :, :], mrow[:, :, :], 1.0, BIG, ALU.subtract, ALU.mult))
        qproj(0, 0)
        pe.wait(t_ctxT, ld_wk)
        t_kT = {}
        for a_ in range(4):
            t = bank.take()
            for side in (0, 64):
                for k in range(2):
                    f = lambda e, t=t, a_=a_, k=k, side=side: e.matmul(
                        t[side:side + 64, 0:2 * TK], wk[:, k, a_ * 64:(a_ + 1) * 64],
                        ctxT[:, k, :, :].rearrange("p b t -> p (b t)"), start=(k == 0), stop=(k == 1))
                    m = pe.done(f) if side and k else pe.run(f)
            act.wait(m, t_bk4)
            if a_ > 1:
                act.wait(t_kT[a_ - 2])
            a = act.done(lambda e, t=t, a_=a_: e.activation(kraw[:, a_ % 2, :], t[:, 0:2 * TK], ACT.Identity, bias=bk4[:, a_:a_ + 1], scale=0.25))
            bank.give(t, a)
            dve.wait(a)
            kr = kraw[:, a_ % 2, :].rearrange("p (b t) -> p b t", b=2)
            d = dve.done(lambda e, a_=a_, kr=kr: e.tensor_copy(kT[:, a_, :, 0, :], kr))
            dve.wait(d)
            t_kT[a_] = dve.done(lambda e, a_=a_, kr=kr: e.tensor_tensor(kT[:, a_, :, 1, :], kr, kT[:, a_, :, 0, :].bitcast(F32), ALU.subtract))

        pe.wait(t_crow, t_idb)
        t = bank.take()
        tb = t[:, :].bitcast(BF16)
        for n in range(8):
            f = lambda e, tb=tb, n=n: e.transpose(tb[0:TK, n * 128:(n + 1) * 128], crow[:, n, :], identb[:, :])
            m = pe.done(f) if n == 7 else pe.run(f)
        dve.wait(m)
        t_cT = dve.done(lambda e, tb=tb: e.tensor_copy(cT[:, :], tb[0:TK, :]))
        bank.give(t, t_cT)

        t_Kb = {}

        def keys(bb, g):
            dve.wait(t_kT[2 * g + 1], *last["Kb_read"].get(g, []))
            for k in range(2 * g, 2 * g + 2):
                t_Kb[bb, g] = dve.done(lambda e, k=k: e.tensor_tensor(
                    Kb[:, k, :, :].rearrange("p l (h t) -> p l h t", t=TK),
                    kT[:, k, bb, :, :].bitcast(F32).unsqueeze(2).to_broadcast([P, 2, 4, TK]),
                    bmask.unsqueeze(1).unsqueeze(3).to_broadcast([P, 2, 4, TK]), ALU.mult))

        t_vsb, t_Vb = {}, {}
        t_wkv_read, t_wo = [], []

        def split_wo():
            act.wait(ld_wo, *t_wkv_read, t_cT)
            m = act.done(lambda e: e.copy(woh[:, :, :], wo[:, :, :]))
            pool.wait(m)
            t_wo.append(pool.done(lambda e: e.tensor_tensor(wol[:, :, :], wo[:, :, :], woh[:, :, :].bitcast(F32), ALU.subtract)))


        def values(bb):
            pe.wait(t_ctxT, ld_wv)
            t = bank.take()
            for k in range(2):
                f = lambda e, t=t, k=k: e.matmul(t[0:TK, 0:E], ctxT[:, k, bb, :], wv[:, k, :], start=(k == 0), stop=(k == 1))
                m = pe.done(f) if k else pe.run(f)
            act.wait(m)
            t_vsb[bb] = act.done(lambda e: e.copy(vsb[:, bb, :], t[0:TK, 0:E]))
            bank.give(t, t_vsb[bb])
            t_wkv_read[:] = [m]

        def pack(bb, j):
            pe.wait(t_vsb[bb], t_rep)
            t = bank.take()
            o = 128 * j % TK
            m = pe.done(lambda e: e.matmul(t[:, 0:E], rep[:, o:o + 128], vsb[:, bb, :], start=True, stop=True))
            dve.wait(m)
            t_Vb[bb] = dve.done(lambda e: e.tensor_tensor(
                Vb[:, bb, j, :].rearrange("p (g h d) -> p g h d", g=2, d=D),
                t[:, 0:E].rearrange("p (g h d) -> p g h d", g=2, d=D),
                vmask[:, 8 * j:8 * j + 8].unsqueeze(1).unsqueeze(3).to_broadcast([P, 2, 8, D]), ALU.mult))
            bank.give(t, t_Vb[bb])

        keys(0, 0)
        t_w1, t_w2 = [], []

        def split(raw, hi, lo, loaded, marks, a, b):
            act.wait(loaded)
            m = act.done(lambda e: e.copy(hi[:, a:b], raw[:, a:b]))
            eng = pool if raw is w1raw else dve
            eng.wait(m)
            marks.append(eng.done(lambda e: e.tensor_tensor(lo[:, a:b], raw[:, a:b], hi[:, a:b].bitcast(F32), ALU.subtract)))

        t_P = {}
        units = [0]

        def scores(i, g):
            c, n, bb = i // 4, i % 4, i // 8
            u = units[0] % 2
            units[0] += 1
            s = S[u]
            pe.wait(t_q[c, g], t_Kb[bb, g], t_cT, t_repb, *last["S_read"].get(u, []))
            for h in range(2):
                for w in range(2):
                    pe.run(lambda e, h=h, w=w: e.matmul(
                        s[:, h, 0:4 * TK], qs[:, 2 * g + h, n * 128:(n + 1) * 128], Kb[:, 2 * g + h, w, :],
                        start=(w == 0), stop=False))
            q0 = (i % 8) * 128
            for h in range(2):
                f = lambda e, h=h: e.matmul(s[:, h, 0:4 * TK], cT[:, q0:q0 + 128], repb[:, :], start=False, stop=True)
                m = pe.done(f) if h else pe.run(f)
            last["q_read"][g] = [m]
            last["Kb_read"][g] = [m]
            sv = s[:, :, 0:4 * TK].rearrange("p b (h t) -> p b h t", t=TK)
            pm = Pm[:, n, g, :]
            p3 = pm.rearrange("p (h t) -> p h t", t=TK)
            dve.wait(m)
            m = dve.done(lambda e: e.tensor_reduce(mx[:, u, :].rearrange("p (b h) -> p b h", b=2), sv, AX_X, ALU.max))
            dve.wait(m, *last["P_read"].get(g, []))
            m = dve.done(lambda e: e.tensor_tensor(
                pm.rearrange("p (b h t) -> p b h t", b=2, t=TK), sv,
                mx[:, u, :].rearrange("p (b h) -> p b h", b=2).unsqueeze(3).to_broadcast([P, 2, 4, TK]), ALU.subtract))
            last["S_read"][u] = [m]

            def exps():
                act.wait(m)
                a = act.done(lambda e: e.activation(pm, pm, ACT.Exp))
                after(LAGS[1], lambda: rest(a))

            def rest(a):
                dve.wait(a)
                m = dve.done(lambda e: e.tensor_reduce(dn[:, u, :], p3, AX_X, ALU.add))
                dve.wait(m, *last["rd"].get(u, []))
                m = dve.done(lambda e: e.reciprocal(rd[:, u, :], dn[:, u, :]))
                pool.wait(m)
                t_P[i, g] = pool.done(lambda e: e.tensor_tensor(p3, p3, rd[:, u, :].unsqueeze(2).to_broadcast([P, 8, TK]), ALU.mult))
                last["rd"][u] = [t_P[i, g]]
            after(LAGS[0], exps)

        t_aT, t_aTh = {}, {}
        pts = [0]
        pend = []

        def pv():
            bb, g, j, slot, a = pend.pop(0)
            pe.wait(a, t_Vb[bb], *(last["acc_read"] if j == 0 else []))
            r = KROWS[j]
            m = pe.done(lambda e: e.matmul(acc[:, :], Vb[0:r, bb, j, g * 128:(g + 1) * 128], PT[0:r, slot, :],
                                           start=(j == 0), stop=(j == 4)))
            last["PT_read"][slot] = [m]
            return m

        def weigh(c, g, j):
            r = KROWS[j]
            t = bank.take()
            for n in range(4):
                pe.wait(t_P[4 * c + n, g])
                f = lambda e, n=n, t=t, r=r, j=j, g=g: e.transpose(t[0:r, n * 128:(n + 1) * 128], Pm[:, n, g, j * 128:j * 128 + r], ident)
                m = pe.done(f) if n == 3 else pe.run(f)
            slot = pts[0] % 4
            pts[0] += 1
            act.wait(m, *last["PT_read"].get(slot, []))
            a = act.done(lambda e, t=t, r=r, slot=slot: e.copy(PT[0:r, slot, :], t[0:r, :]))
            bank.give(t, a)
            pend.append((c // 2, g, j, slot, a))
            if j == 4:
                last["P_read"][g] = [m]

        def weigh_end(c, g):
            m = pv()
            act.wait(m, *last["aT_read"])
            a = act.done(lambda e: e.activation(aT[:, g, :], acc[:, :], ACT.Identity, bias=cols[:, 6 + g:7 + g]))
            dve.wait(a, *t_wkv_read)
            t_aTh[c, g] = a
            a = dve.done(lambda e: e.scalar_tensor_tensor(
                aTl[:, g, :], acc[:, :], cols[:, 6 + g:7 + g], aT[:, g, :].bitcast(F32), ALU.add, ALU.subtract))
            last["acc_read"] = [a]
            t_aT[c, g] = a

        t_x2 = {}
        t_n2 = {}
        t_x2T = {}

        def out_norm2(c):
            st, mv, ve, rs = stats[1]
            assert (c, 1) in t_aT
            pe.wait(t_wo[0])
            for h in range(2):
                t = bank.take()
                for n in range(2):
                    q = (2 * h + n) * 128
                    parts = [(k, y, w) for k in range(2) for y, w in ((aT, woh), (aT, wol), (aTl, woh))]
                    for p_, (k, y, w) in enumerate(parts):
                        pe.wait((t_aTh if y is aT else t_aT)[c, k])
                        f = lambda e, t=t, n=n, q=q, k=k, y=y, w=w, p_=p_: e.matmul(
                            t[:, n * E:(n + 1) * E], y[:, k, q:q + 128], w[:, k, :], start=(p_ == 0), stop=(p_ == 5))
                        m = pe.done(f) if n and p_ == 5 else pe.run(f)
                dve.wait(m, t_xb[c], *t_w2, *last["x1_read"].get(c % 2, []))
                d = dve.done(lambda e, t=t, h=h: e.tensor_tensor(
                    x1[:, c % 2, 2 * h:2 * h + 2, :].rearrange("p n e -> p (n e)"), t[:, :],
                    xin[:, 4 * c + 2 * h:4 * c + 2 * h + 2, :].rearrange("p n e -> p (n e)"), ALU.add))
                bank.give(t, d)
                dve.wait(d)
                for n in range(2):
                    s = dve.done(lambda e, h=h, n=n: e.bn_stats(st[:, 2 * h + n, :], x1[:, c % 2, 2 * h + n, :]))
            last["aT_read"] = [m]
            r = rstd(1, s)

            def scale():
                dve.wait(r, *t_w1, *last["xn2_read"].get(c % 2, []))
                for n in range(4):
                    m = dve.done(lambda e, n=n: e.tensor_scalar(
                        xn2[:, c % 2, n, :], x1[:, c % 2, n, :], mv[:, n, 0:1], rs[:, n:n + 1], ALU.subtract, ALU.mult))
                t_n2[c] = m
            after(LAGS[3], scale)

        def turn2(c):
            pe.wait(t_n2[c])
            for k in range(2):
                t = bank.take()
                for n in range(4):
                    f = lambda e, n=n, t=t, k=k: e.transpose(t[:, n * 128:(n + 1) * 128], xn2[:, c % 2, n, k * 128:(k + 1) * 128], ident)
                    m = pe.done(f) if n == 3 else pe.run(f)
                act.wait(m, *last["x2_read"])
                a = act.done(lambda e, t=t, k=k: e.copy(x2h[:, k, :], t[:, :]))
                dve.wait(a)
                d = dve.done(lambda e, t=t, k=k: e.tensor_tensor(x2l[:, k, :], t[:, :], x2h[:, k, :].bitcast(F32), ALU.subtract))
                bank.give(t, d)
            t_x2[c] = d
            t_x2T[c] = [m]

        def biases2(c):
            pool.wait(*t_x2T[c], ld_b2, ld_be)
            for n in range(0, 4, 2):
                for y, v in ((xn2, b2_r), (x1, be_r)):
                    yy = y[:, c % 2, n:n + 2, :]
                    vv = v[:, :].unsqueeze(1).to_broadcast([P, 2, E])
                    p = pool.done(lambda e, yy=yy, vv=vv: e.tensor_tensor(yy, yy, vv, ALU.add))
            t_x1b[c] = p

        t_x1b = {}
        t_h = {}

        def ffn1(c, f_):
            pe.wait(t_x2[c], *t_w1)
            t = bank.take()
            n = 0
            for k in range(2):
                o = k * F + f_ * 128
                for w, y in ((w1h, x2h), (w1h, x2l), (w1l, x2h)):
                    f = lambda e, w=w, y=y, n=n, o=o, k=k, t=t: e.matmul(t[:, :], w[:, o:o + 128], y[:, k, :], start=(n == 0), stop=(n == 5))
                    m = pe.done(f) if n == 5 else pe.run(f)
                    n += 1
            if f_ == 7:
                last["x2_read"] = [m]
            r = f_ % 2
            act.wait(m, *last["hr_read"].get(r, []))
            a = act.done(lambda e, t=t, r=r: e.activation(hr[:, r, :], t[:, :], ACT.Relu, bias=cols[:, 8 + f_:9 + f_]))
            bank.give(t, a)
            act.wait(a, *last["h_read"])
            d = act.done(lambda e, r=r: e.copy(hh[:, f_, :], hr[:, r, :]))
            eng = pool if f_ % 2 and c < NC - 1 else dve

            def low():
                eng.wait(d)
                m = eng.done(lambda e: e.tensor_tensor(hl[:, f_, :], hr[:, r, :], hh[:, f_, :].bitcast(F32), ALU.subtract))
                last["hr_read"][r] = [m]
                t_h[c, f_] = (d, m)
            after(LAGS[2], low)

        s_out = [sem("stored0"), sem("stored1")]
        stores = [0, 0]

        open2 = {}

        def ffn2(c, h, part):
            pe.wait(*t_w2)
            if part == 0 or c == NC - 1 and part == 2:
                open2[h] = bank.take()
            t = open2[h]
            n = part // 2
            q = (2 * h + n) * 128
            cnt = 12 * (part % 2)
            for f_ in range(4 * (part % 2), 4 * (part % 2) + 4):
                for y, w in ((hh, w2h), (hh, w2l), (hl, w2h)):
                    pe.wait(t_h[c, f_][y is hl])
                    f = lambda e, y=y, w=w, f_=f_, q=q, n=n, cnt=cnt, t=t: e.matmul(
                        t[:, n * E:(n + 1) * E], y[:, f_, q:q + 128], w[:, f_ * E:(f_ + 1) * E], start=(cnt == 0), stop=(cnt == 23))
                    m = pe.done(f) if cnt == 23 else pe.run(f)
                    cnt += 1
            if part == 3 and h == 1:
                last["h_read"] = [m]
            if c < NC - 1 and part == 3:
                result(c, h, t, m, 0, 2)
            if c == NC - 1 and part % 2:
                result(c, h, t, m, n, n + 1)

        def result(c, h, t, m, na, nb):
            u = h
            st, mv, ve, rs = stats[2 + u]
            k = nb - na
            y = yb[:, u, na:nb, :]
            dve.wait(m, t_x1b[c], *last["ob_read"].get(u, []))
            d = dve.done(lambda e: e.tensor_tensor(
                y.rearrange("p n e -> p (n e)"), t[:, na * E:nb * E],
                xn2[:, c % 2, 2 * h + na:2 * h + nb, :].rearrange("p n e -> p (n e)"), ALU.add))
            bank.give(t, d)
            if nb == 2:
                last["xn2_read"][c % 2] = [d]
            dve.wait(d)
            for n in range(na, nb):
                s = dve.done(lambda e, n=n: e.bn_stats(st[:, n, :], yb[:, u, n, :]))
            after(LAGS[3], lambda: root(s))

            def root(s):
                r = rstd(2 + u, s, na, nb)
                after(LAGS[3], lambda: finish(r))

            def finish(r):
                dve.wait(r, ld_ga)
                for n in range(na, nb):
                    s = dve.done(lambda e, n=n: e.scalar_tensor_tensor(
                        yb[:, u, n, :], yb[:, u, n, :], mv[:, n, 0:1], ga_r[:, :], ALU.subtract, ALU.mult))
                for n in range(na, nb):
                    if n == na:
                        dve.wait(s)
                    t_y = dve.done(lambda e, n=n: e.scalar_tensor_tensor(
                        yb[:, u, n, :], yb[:, u, n, :], rs[:, n:n + 1], x1[:, c % 2, 2 * h + n, :], ALU.mult, ALU.add))
                s = t_y
                last["x1_read"][c % 2] = [s]
                sp.wait(s)
                n0 = 4 * c + 2 * h + na
                sp.run(lambda e: e.dma_start(o_v[:, n0:n0 + k, :], y).then_inc(s_out[u], 16))
                stores[u] += 1
                if c < NC - 1:
                    last["ob_read"][u] = [(s_out[u], 16 * stores[u])]

        def score_piece(c, n, g):
            scores(4 * c + n, g)

        def weave(*plans):
            pieces = [(at, k, what) for k, plan in enumerate(plans) for at, what in plan]
            for _, _, what in sorted(pieces, key=lambda p: (p[0], p[1])):
                what()
                tick()

        def spread(a, b, whats):
            return [(a + (b - a) * k / len(whats), w) for k, w in enumerate(whats)]

        def later(f, *args):
            return lambda: f(*args)

        def score_plan(b, c, g):
            return spread(0, b, [later(score_piece, c, n, g) for n in range(4)])

        def weigh_plan(a, b, lag, c, g):
            step = (b - a) / 5
            return ([(a, drain)] + [(a + step * j, later(weigh, c, g, j)) for j in range(5)]
                    + [(a + step * (j + lag), pv) for j in range(4)] + [(a + step * (4 + lag), later(weigh_end, c, g))])

        def ffn1_plan(a, b, c):
            return spread(a, b, [later(ffn1, c, f_) for f_ in range(8)])

        def ffn2_plan(a, b, c):
            return spread(a, b, [later(ffn2, c, h, part) for h in range(2) for part in range(4)])

        def split_plan(a, b):
            return spread(a, b, [later(split, *w, 512 * k, 512 * k + 512) for w in (
                (w1raw, w1h, w1l, ld_w1, t_w1), (w2raw, w2h, w2l, ld_w2, t_w2)) for k in range(4)])

        weave(spread(0, 1, [later(score_piece, 0, n, 0) for n in range(4)]),
              [(C[0], later(values, 0)), (C[0], later(values, 1))] + spread(C[0], C[1], [later(pack, 0, j) for j in range(5)]),
              [(C[6], later(qproj, 0, 1)), (C[2], later(norm1, 1)), (C[3], later(keys, 0, 1))])
        drain()
        for c in range(NC + 1):
            a, b = A[10 * (c < 2):], B[10 * (c < 1):]
            if c:
                plans = [weigh_plan(a[0], a[1], a[7], c - 1, 1), [(a[2], later(out_norm2, c - 1)), (a[3], later(turn2, c - 1))]]
                if c < NC:
                    plans.append(score_plan(a[8], c, 0))
                    plans.append([(0.0, later(qproj, c, 1))])
                if c > 1:
                    plans.append(ffn2_plan(a[4], a[5], c - 2))
                if c == NC:
                    plans.append([(0.99, later(biases2, c - 1))])
                if c == 2:
                    plans.append([(0.0, later(keys, 1, 1))])
                if c == 1:
                    plans.append(spread(C[4], C[5], [later(pack, 1, j) for j in range(5)]))
                weave(*plans)
            if c < NC:
                plans = [score_plan(b[9], c, 1), weigh_plan(b[0], b[1], b[8], c, 0)]
                if c == 1:
                    plans.append([(0.9, later(keys, 1, 0))])
                if c == 0:
                    plans.append(split_plan(b[2], b[3]))
                    plans.append([(b[4], later(xbias, 0)), (0.3, split_wo)])
                if c:
                    plans.append(ffn1_plan(b[2], b[3], c - 1))
                    plans.append([(b[4], later(biases2, c - 1))])
                if c + 1 < NC:
                    if c + 2 < NC:
                        plans.append([(a[6], later(norm1, c + 2))])
                    plans.append([(b[5], later(turn1, c + 1)), (b[6], later(qproj, c + 1, 0)), (b[7], later(xbias, c + 1))])
                weave(*plans)
        for f_ in range(8):
            ffn1(NC - 1, f_)
            tick()
        drain()
        for h in range(2):
            for part in range(4):
                ffn2(NC - 1, h, part)
                tick()
        drain()
        sp.wait(*((s_out[u], 16 * stores[u]) for u in range(2)))

        block = stack.enter_context(nc.Block())
        block.sync(sp.play)
        block.scalar(act.play)
        block.vector(dve.play)
        block.gpsimd(pool.play)
        block.tensor(pe.play)


_INS = ["x", "ctx_1024", "mask_1x1xSxS2_fk0", "L0_xattn_Wq", "L0_xattn_bq", "L0_xattn_Wk", "L0_xattn_bk",
        "L0_xattn_Wv", "L0_xattn_bv", "L0_xattn_Wo", "L0_xattn_bo", "L0_ffn_w1", "L0_ffn_b1", "L0_ffn_w2",
        "L0_ffn_b2", "L0_ffn_gamma", "L0_ffn_beta"]


def _constants():
    c = np.zeros((128, 172), np.float32)
    p = np.arange(128)
    c[p, p] = 1.0
    c[p, 128 + p % 64 // 16] = 1.0
    for j in range(5):
        h = (128 * j + p) // 77
        ok = h < 8
        c[p[ok], 132 + 8 * j + h[ok]] = 1.0
    return c


def kernel(**inputs):
    import numpy as _np
    import concourse.bacc as _bacc
    from concourse import mybir as _mybir
    from concourse.bass_utils import run_bass_kernel_spmd as _run

    nc = _bacc.Bacc("TRN2", target_bir_lowering=False, num_devices=1)
    arrays, args = {}, []
    for name in _INS + ["const"]:
        a = _constants() if name == "const" else _np.ascontiguousarray(inputs[name])
        arrays[f"in_{name}_dram"] = a
        args.append(nc.dram_tensor(f"in_{name}_dram", a.shape, _mybir.dt.from_np(a.dtype), kind="ExternalInput").ap())
    out = nc.dram_tensor("out_0_dram", (2, 1024, 256), F32, kind="ExternalOutput").ap()
    build(nc, *args, out)
    r = _run(nc, [arrays], core_ids=[0])
    return r.results[0]["out_0_dram"]
```
